# Optimizing a Trainium2 kernel written in Bass

```python
import numpy as np
import jax
import jax.numpy as jnp

def _softmax(x, axis=-1):
    return jax.nn.softmax(x, axis=axis)

def _gelu(x):
    return jax.nn.gelu(x, approximate=True)

def _silu(x):
    return jax.nn.silu(x)

def _sigmoid(x):
    return jax.nn.sigmoid(x)

def _layernorm(x, axis=-1, eps=1e-05):
    m = jnp.mean(x, axis=axis, keepdims=True)
    v = jnp.var(x, axis=axis, keepdims=True)
    return (x - m) / jnp.sqrt(v + eps)

def _scatter_add(tgt, idx, src, axis=0):
    return tgt.at[idx].add(src)

def _segment_sum(src, seg, n):
    return jax.ops.segment_sum(src, seg, n)
kernel_name = 'mk_seq_preln_d1_jaxref_r8_fe7940'

def setup_inputs(seed: int=0):
    np.random.seed(seed)
    _w = jnp.asarray

    def _L0_attn_setup():
        import jax, jax.numpy as jnp
        import numpy as np
        EMBED_DIM = 128
        NUM_HEADS = 16
        HEAD_DIM = EMBED_DIM // NUM_HEADS
        key = jax.random.key(seed)
        k1, k2, k3 = jax.random.split(key, 3)
        inputs = jax.random.normal(k1, (4, 256, EMBED_DIM), dtype=jnp.float32)
        rotation_params = jax.random.normal(k2, (NUM_HEADS, HEAD_DIM), dtype=jnp.float32)
        entangle_params = jax.random.normal(k3, (NUM_HEADS, HEAD_DIM), dtype=jnp.float32)
        return {'inputs': inputs, 'rotation_params': rotation_params, 'entangle_params': entangle_params}
    _L0_attn_in = _L0_attn_setup()

    def _L0_ffn_setup():
        import jax, jax.numpy as jnp
        import numpy as np

        def _bitlinear(x, w_latent):
            scale = jax.lax.stop_gradient(jnp.clip(jnp.mean(jnp.abs(w_latent), axis=1, keepdims=True), 1e-05, None))
            tern = jnp.clip(jnp.round(w_latent / scale), -1.0, 1.0)
            w = w_latent + jax.lax.stop_gradient(tern - w_latent)
            return x @ (w * scale).T
        key = jax.random.key(seed)
        ks = jax.random.split(key, 6)
        dim, hidden, rank = (128, 512, 16)
        B, S = (4, 512)
        x = jax.random.normal(ks[0], (B, S, dim), dtype=jnp.float32)
        w_fc = 0.02 * jax.random.normal(ks[1], (hidden, dim), dtype=jnp.float32)
        w_proj = 0.02 * jax.random.normal(ks[2], (dim, hidden), dtype=jnp.float32)
        u = 0.02 * jax.random.normal(ks[3], (hidden, rank), dtype=jnp.float32)
        v = 0.02 * jax.random.normal(ks[4], (rank, dim), dtype=jnp.float32)
        fast_b = jax.random.normal(ks[5], (rank, rank), dtype=jnp.float32)
        gate = jnp.float32(0.05)
        return {'x': x, 'fast_b': fast_b, 'w_fc': w_fc, 'w_proj': w_proj, 'u': u, 'v': v, 'gate': gate}
    _L0_ffn_in = _L0_ffn_setup()
    _d = {'L0_attn_inputs': _L0_attn_in['inputs'], 'L0_attn_rotation_params': _L0_attn_in['rotation_params'], 'L0_attn_entangle_params': _L0_attn_in['entangle_params'], 'L0_ffn_fast_b': _L0_ffn_in['fast_b'], 'L0_ffn_w_fc': _L0_ffn_in['w_fc'], 'L0_ffn_w_proj': _L0_ffn_in['w_proj'], 'L0_ffn_u': _L0_ffn_in['u'], 'L0_ffn_v': _L0_ffn_in['v'], 'L0_ffn_gate': _L0_ffn_in['gate']}
    _x0 = _d['L0_attn_inputs']
    _d['L0_attn_inputs'] = jax.random.normal(jax.random.fold_in(jax.random.key(seed), 1), (4, 1024, 128), dtype=_x0.dtype)
    del _x0
    return _d

def reference(L0_attn_inputs, L0_attn_rotation_params, L0_attn_entangle_params, L0_ffn_fast_b, L0_ffn_w_fc, L0_ffn_w_proj, L0_ffn_u, L0_ffn_v, L0_ffn_gate):

    def _L0_attn_ref(inputs, rotation_params, entangle_params):
        import jax, jax.numpy as jnp
        import numpy as np
        EMBED_DIM = 128
        NUM_HEADS = 16
        HEAD_DIM = EMBED_DIM // NUM_HEADS
        B, T, _ = inputs.shape
        x = inputs.reshape(B, T, NUM_HEADS, HEAD_DIM).transpose(0, 2, 1, 3)
        q = x * rotation_params[None, :, None, :]
        k = x * entangle_params[None, :, None, :]
        v = x
        scale = 1.0 / np.sqrt(HEAD_DIM).astype(np.float32)
        attn_scores = jnp.einsum('bhid,bhjd->bhij', q, k) * scale
        attn_weights = jax.nn.softmax(attn_scores, axis=-1)
        out = jnp.einsum('bhij,bhjd->bhid', attn_weights, v)
        out = out.transpose(0, 2, 1, 3).reshape(B, T, EMBED_DIM)
        return out

    def _L0_ffn_ref(x, fast_b, w_fc, w_proj, u, v, gate):
        import jax, jax.numpy as jnp
        import numpy as np

        def _bitlinear(x, w_latent):
            scale = jax.lax.stop_gradient(jnp.clip(jnp.mean(jnp.abs(w_latent), axis=1, keepdims=True), 1e-05, None))
            tern = jnp.clip(jnp.round(w_latent / scale), -1.0, 1.0)
            w = w_latent + jax.lax.stop_gradient(tern - w_latent)
            return x @ (w * scale).T
        h = _bitlinear(x, w_fc) + gate * (x @ v.T @ fast_b.T @ u.T)
        r = jnp.maximum(h, 0.0)
        return _bitlinear(r * r, w_proj)
    x = L0_attn_inputs
    x = x + _L0_attn_ref(_layernorm(x, axis=-1), L0_attn_rotation_params, L0_attn_entangle_params)
    x = x + _L0_ffn_ref(_layernorm(x, axis=-1), L0_ffn_fast_b, L0_ffn_w_fc, L0_ffn_w_proj, L0_ffn_u, L0_ffn_v, L0_ffn_gate)
    return x

_drawn_inputs = setup_inputs


def setup_inputs(seed=0):
    import zlib

    import numpy as np

    out = dict(_drawn_inputs(seed))
    spreads = {}
    factors = {'L0_ffn_fast_b': 8.0,
     'L0_ffn_w_fc': 5.756,
     'L0_ffn_w_proj': 4.62,
     'L0_ffn_u': 8.0,
     'L0_ffn_v': 8.0}
    for name, (base, spread) in spreads.items():
        noise = np.random.default_rng([zlib.crc32(name.encode()), seed]).standard_normal(out[name].shape)
        drawn = base * np.exp(spread * noise) if base else spread * noise
        out[name] = jnp.asarray(drawn.astype(out[name].dtype))
    for name, factor in factors.items():
        out[name] = (out[name] * factor).astype(out[name].dtype)
    return out
```

```python
from contextlib import ExitStack

import concourse.bass as bass
from concourse import mybir

F32, BF16, I32 = mybir.dt.float32, mybir.dt.bfloat16, mybir.dt.int32
ACT = mybir.ActivationFunctionType
ALU = mybir.AluOpType
AX_X = mybir.AxisListType.X

B, T, C, H = 4, 1024, 128, 16
D = C // H
P = 128
TILES = T // P
HG = 4
GROUPS = B * H // HG
STEPS = GROUPS // 2
HALF = 512
PARTS = 6
ROWS = 6 * D
SROWS = ROWS + 3
VW = 32
HID, RANK = 512, 16
HC = HID // P
FT = 2
EPS = 1e-5
SHIFT_LIMIT = 32.0
MAGIC = float(0x5F3759DF)
LAG = 4


def build(nc, x_in, rot, ent, fast_b, w_fc, w_proj, u_in, v_in, gate, out):
    q_dram = nc.dram_tensor("q_scratch", (B * C, 6, T), BF16, kind="Internal").ap()
    k_dram = nc.dram_tensor("k_scratch", (B * C, 6, T), BF16, kind="Internal").ap()
    shift_dram = nc.dram_tensor("shift_scratch", (B * H, 3, T), BF16, kind="Internal").ap()

    with ExitStack() as ctx:
        def sb(name, shape, dt=F32):
            return ctx.enter_context(nc.sbuf_tensor(name, shape, dt))

        def sem(name):
            return ctx.enter_context(nc.semaphore(name))

        psum = ctx.enter_context(nc.psum_tensor("psum", [P, 4096], F32))
        score_ps = [psum[:, 0:1024], psum[:, 1024:2048]]
        o_ps = psum[:, 2048:3072]
        aux_ps = psum[:, 3072:4096]

        X = sb("X", [P, B * TILES, C])
        XN = sb("XN", [P, B * TILES, C])
        normed = sb("normed", [P, TILES, C])
        split = sb("split", [P, PARTS, T], BF16)
        wx = sb("wx", [P, T])
        rest_k = sb("rest_k", [P, T])
        rest_q = sb("rest_q", [P, T])
        bound_in = sb("bound_in", [P, T], BF16)
        shift_rows = sb("shift_rows", [H, B, 3, T], BF16)
        QT = [sb(f"QT{k}", [P, 2, T], BF16) for k in range(2)]
        KT = [sb(f"KT{k}", [P, 2, T], BF16) for k in range(2)]
        V = [sb(f"V{k}", [P, TILES, HG, VW]) for k in range(2)]
        E = sb("E", [P, 2, HG, T])
        o_sb = sb("o_sb", [P, T])
        att = sb("att", [P, TILES, HG, D])
        rden = sb("rden", [P, TILES, HG])
        bn = sb("bn", [P, B * TILES, 6])
        mv = sb("mv", [P, B * TILES, 2])
        var = sb("var", [P, B * TILES])
        rstd = sb("rstd", [P, B * TILES])
        nt = sb("nt", [P, B * TILES])
        fbn, fmv = sb("fbn", [P, FT, 6]), sb("fmv", [P, FT, 2])
        fvar, frstd, fnt = sb("fvar", [P, FT]), sb("frstd", [P, FT]), sb("fnt", [P, FT])
        fn = sb("fn", [P, FT, C])
        fT = sb("fT", [P, FT * P])
        relu = sb("relu", [P, HC, FT * P])
        relu2 = sb("relu2", [P, HC, FT * P])
        y = [sb(f"y{k}", [P, FT, C]) for k in range(2)]
        ident = sb("ident", [P, P])
        head_of = sb("head_of", [P, H], BF16)
        signed_head = sb("signed_head", [P, H], BF16)
        rot_c, ent_c, w_c, sgn_c = (sb(n, [P, 1]) for n in ("rot_c", "ent_c", "w_c", "sgn_c"))
        neg_c = sb("neg_c", [P, 1])
        credit = sb("credit", [P, 8])
        cmax = sb("cmax", [H, B])
        cneg = sb("cneg", [H, B])
        call = sb("call", [H, 1])
        call1 = sb("call1", [1, 1])
        flag = sb("flag", [1, 1], I32)
        zrow = sb("zrow", [H, T], BF16)
        wfc = sb("wfc", [P, HC, C])
        wpj = sb("wpj", [P, HID])
        wa, wb = sb("wa", [P, 512]), sb("wb", [P, 512])
        ws, wh = sb("ws", [P, HC]), sb("wh", [P, HC])
        wnh = sb("wnh", [P, HC])
        u_sb = sb("u_sb", [P, HC, RANK])
        v_sb = sb("v_sb", [RANK, C])
        fb_sb = sb("fb_sb", [RANK, RANK])
        fbT = sb("fbT", [RANK, RANK])
        fbv = sb("fbv", [RANK, C])
        uT = sb("uT", [RANK, HID])
        gate_c = sb("gate_c", [RANK, 1])
        W1 = sb("W1", [P, HID])
        W2 = sb("W2", [P, HC, C])
        rmax = sb("rmax", [P, HG, TILES])
        nmax = sb("nmax", [HG * TILES, P])
        nres = sb("nres", [HG * TILES, P])
        nparts = sb("nparts", [HG * TILES, 3, P], BF16)

        s_x = [sem(f"s_x{b}") for b in range(B)]
        s_w = sem("s_weights_loaded")
        s_wc = sem("s_rot_ent_loaded")
        s_const = sem("s_constants")
        s_preset = sem("s_operands_preset")
        s_norm = sem("s_normed")
        s_xt = sem("s_x_transposed")
        s_split = sem("s_act_split")
        s_rest = sem("s_rest")
        s_klow = sem("s_k_low_part")
        s_qlow = sem("s_q_low_part")
        s_bin = sem("s_bound_in")
        s_bmm = sem("s_bound_product")
        s_xn = sem("s_xn_stored")
        s_parts = sem("s_parts_stored")
        s_bound = sem("s_bound")
        s_shr = sem("s_shift_rows")
        s_shift = sem("s_shift_stored")
        s_flag_t = sem("s_flag_transposed")
        s_flag = sem("s_flag")
        s_qk = [sem(f"s_qk{k}") for k in range(2)]
        s_v = [sem(f"s_v{k}") for k in range(2)]
        s_S = sem("s_scores")
        s_E = sem("s_exps")
        s_pv = sem("s_pv")
        s_ev = sem("s_o_evacuated")
        s_to = sem("s_o_transposed")
        s_att = sem("s_attention_read")
        s_fTc = sem("s_ffn_transposed_copied")
        s_fn = sem("s_ffn_normed")
        s_fT = sem("s_ffn_transposed")
        s_fc = sem("s_ffn_hidden")
        s_relu = sem("s_ffn_relu")
        s_relu2 = sem("s_ffn_relu2")
        s_fp = sem("s_ffn_projected")
        s_y = sem("s_y")
        s_out = [sem(f"s_out_stored{k}") for k in range(2)]
        s_wt = sem("s_weights_product")
        s_wd = sem("s_weights_copied")
        c_pre, c_general, c_first, c_mid, c_weights, c_last, c_tail = (
            sem(f"c_{n}") for n in ("pre", "general", "first", "mid", "weights", "last", "tail"))
        m_load = sem("m_operands_loaded")
        m_S = sem("m_scores")
        m_max = sem("m_max")
        m_t = sem("m_max_transposed")
        m_parts = sem("m_max_parts")
        m_store = sem("m_shift_stored")

        def load_group(sp, first, k, done):
            for r in range(2):
                rows = 64 * r
                for pair in range(2):
                    head = first + r + 2 * pair
                    for dst, src in ((QT[k], q_dram), (KT[k], k_dram)):
                        sp.dma_start(dst[rows:rows + ROWS, pair, :],
                                     src[bass.ds(D * head, D), :, :].rearrange("d t n -> (d t) n")).then_inc(done, 16)
                    sp.dma_start(QT[k][rows + ROWS:rows + SROWS, pair, :],
                                 shift_dram[bass.ds(head, 1), :, :].rearrange("h p n -> (h p) n")).then_inc(done, 16)

        LOADED = 12 * 16

        def out_rows(chunk):
            return out.rearrange("b t c -> (b t) c")[bass.ds(chunk * (FT * P), FT * P), :].rearrange("(t p) c -> p t c", p=P)

        block = ctx.enter_context(nc.Block())

        @block.sync
        def _(sp):
            sp.dma_start(rot_c[:, :], rot.rearrange("h (d o) -> (h d) o", o=1)).then_inc(s_wc, 16)
            sp.dma_start(ent_c[:, :], ent.rearrange("h (d o) -> (h d) o", o=1)).then_inc(s_wc, 16)
            for b in range(B):
                sp.dma_start(X[:, TILES * b:TILES * (b + 1), :],
                             x_in[b].rearrange("(t p) c -> p t c", p=P)).then_inc(s_x[b], 16)
            sp.dma_start(wfc[:, :, :], w_fc.rearrange("(t p) c -> p t c", p=P)).then_inc(s_w, 16)
            sp.dma_start(wpj[:, :], w_proj).then_inc(s_w, 16)
            sp.dma_start(u_sb[:, :, :], u_in.rearrange("(t p) r -> p t r", p=P)).then_inc(s_w, 16)
            sp.dma_start(v_sb[:, :], v_in).then_inc(s_w, 16)
            sp.dma_start(fb_sb[:, :], fast_b).then_inc(s_w, 16)
            sp.dma_start(gate_c[:, :], gate.rearrange("(a b) -> a b", a=1).to_broadcast([RANK, 1])).then_inc(s_w, 16)
            with sp.Fori(0, B) as b:
                sp.wait_ge(s_norm, b + 1)
                sp.dma_start(XN[:, bass.ds(TILES * b, TILES), :], normed[:, :, :]).then_inc(s_xn, 16)
                sp.wait_ge(s_split, 5 * b + 5)
                sp.wait_ge(s_klow, b + 1)
                sp.wait_ge(s_qlow, b + 1)
                rows = bass.ds(C * b, C)
                sp.dma_start(q_dram[rows, 0:3, :], split[:, 0:3, :]).then_inc(s_parts, 16)
                sp.dma_start(q_dram[rows, 3:5, :], split[:, 0:2, :]).then_inc(s_parts, 16)
                sp.dma_start(q_dram[rows, 5:6, :], split[:, 0:1, :]).then_inc(s_parts, 16)
                sp.dma_start(k_dram[rows, 0:3, :], split[:, 3:4, :].to_broadcast([P, 3, T])).then_inc(s_parts, 16)
                sp.dma_start(k_dram[rows, 3:5, :], split[:, 4:5, :].to_broadcast([P, 2, T])).then_inc(s_parts, 16)
                sp.dma_start(k_dram[rows, 5:6, :], split[:, 5:6, :]).then_inc(s_parts, 16)
            sp.wait_ge(s_parts, 16 + 16 * PARTS * B)
            sp.wait_ge(s_shr, 1)
            sp.dma_start(shift_dram.rearrange("(b h) p n -> h b (p n)", b=B),
                         shift_rows[:, :, :, :].rearrange("h b p n -> h b (p n)")).then_inc(s_shift, 16)
            sp.wait_ge(s_shift, 16)
            sp.wait_ge(s_preset, 1)
            sp.wait_ge(s_flag, 1)
            general = sp.value_load(flag[0:1, 0:1], min_val=0, max_val=1)
            with sp.If(general == 1):
                with sp.Fori(0, GROUPS) as g:
                    sp.wait_ge(m_store, 16 * HG * g + 64)
                    load_group(sp, HG * g, 0, m_load)
                    sp.wait_ge(m_parts, g + 1)
                    for h in range(HG):
                        sp.dma_start(
                            shift_dram[bass.ds(HG * g + h, 1), :, :].rearrange("h p (t n) -> (h t) p n", n=P),
                            nparts[TILES * h:TILES * (h + 1), :, :]).then_inc(m_store, 16)
                sp.wait_ge(m_store, 16 * HG * GROUPS + 64)
            load_group(sp, 0, 0, s_qk[0])
            load_group(sp, HG, 1, s_qk[1])

            def next_load(s, k):
                sp.wait_ge(s_S, 64 * s + 32 * k - 32)
                load_group(sp, 8 * s + HG * k, k, s_qk[k])

            def store(chunk, k):
                sp.wait_ge(s_y, chunk + 1)
                sp.dma_start(out_rows(chunk), y[k][:, :, :]).then_inc(s_out[k], 16)

            with sp.Fori(1, 3) as s:
                for k in range(2):
                    next_load(s, k)
            with sp.Fori(3, STEPS) as s:
                for k in range(2):
                    next_load(s, k)
                    store(2 * s + k - 6, k)
            with sp.Fori(STEPS, STEPS + 3) as s:
                for k in range(2):
                    store(2 * s + k - 6, k)
            for k in range(2):
                sp.wait_ge(s_out[k], 16 + 16 * STEPS)

        @block.gpsimd
        def _(pool):
            nc.gpsimd.memset(ident[:, :], 0.0).then_inc(s_const, 1)
            nc.gpsimd.memset(head_of[:, :], 1.0).then_inc(s_const, 1)
            pool.wait_ge(s_const, 2)
            nc.gpsimd.affine_select(out=ident[:, :], in_=ident[:, :], compare_op=ALU.not_equal, fill=1.0,
                                    base=0, pattern=[[-1, P]], channel_multiplier=1).then_inc(s_const, 1)
            nc.gpsimd.affine_select(out=head_of[:, :], in_=head_of[:, :], compare_op=ALU.is_ge, fill=0.0,
                                    base=0, pattern=[[-D, H]], channel_multiplier=1).then_inc(s_const, 1)
            pool.wait_ge(s_const, 4)
            nc.gpsimd.affine_select(out=head_of[:, :], in_=head_of[:, :], compare_op=ALU.is_ge, fill=0.0,
                                    base=D - 1, pattern=[[D, H]], channel_multiplier=-1).then_inc(s_const, 1)
            nc.gpsimd.memset(zrow[:, :], 0.0).then_inc(s_const, 1)
            nc.gpsimd.memset(V[0][:, :, :, :], 0.0)
            nc.gpsimd.memset(V[1][:, :, :, :], 0.0).then_inc(s_v[1], 1)
            pool.wait_ge(s_v[1], 1)
            nc.gpsimd.memset(V[0][:, :, :, D:D + 1], 1.0)
            nc.gpsimd.memset(V[1][:, :, :, D:D + 1], 1.0).then_inc(s_v[1], 1)
            nc.gpsimd.memset(shift_rows[:, :, :, :], 0.0)
            for k in range(2):
                last = nc.gpsimd.memset(KT[k][:, :, :], 1.0)
            last.then_inc(s_preset, 1)
            with pool.Fori(0, B) as b:
                pool.wait_ge(s_split, 5 * b + 2)
                nc.gpsimd.tensor_tensor(out=bound_in[:, :], in0=wx[:, :], in1=split[:, 3, :],
                                        op=ALU.mult).then_inc(s_bin, 1)
                pool.wait_ge(s_split, 5 * b + 5)
                nc.gpsimd.tensor_tensor(out=split[:, 2, :], in0=rest_q[:, :], in1=split[:, 1, :],
                                        op=ALU.subtract).then_inc(s_qlow, 1)
            pool.wait_ge(s_xn, 16 + 16 * B)

            def values(step, k):
                nc.gpsimd.tensor_copy(
                    V[k][:, :, :, 0:D],
                    XN[:, bass.ds(TILES * (step // 2), TILES), bass.ds(64 * (step % 2) + 32 * k, HG * D)]
                    .rearrange("p t (h d) -> p t h d", d=D)).then_inc(s_v[k], 1)

            def square(chunk):
                pool.wait_ge(s_relu, chunk + 1)
                nc.gpsimd.tensor_tensor(out=relu2[:, :, :], in0=relu[:, :, :], in1=relu[:, :, :],
                                        op=ALU.mult).then_inc(s_relu2, 1)

            pool.wait_ge(s_v[1], 2)
            values(0, 0)
            values(0, 1)
            with pool.Fori(1, 3) as s:
                for k in range(2):
                    pool.wait_ge(s_pv, 32 * s + 16 * k - 16)
                    values(s, k)
            with pool.Fori(2, STEPS - 1) as s:
                for k in range(2):
                    square(2 * s + k - LAG)
                    pool.wait_ge(s_pv, 32 * s + 16 * k + 16)
                    values(s + 1, k)
            for k in range(2):
                square(2 * STEPS - 2 + k - LAG)
            with pool.Fori(GROUPS - LAG, GROUPS) as chunk:
                square(chunk)

        @block.scalar
        def _(act):
            with act.Fori(0, B) as b:
                act.wait_ge(s_parts, 16 * PARTS * b + 16)
                act.wait_ge(s_xt, b + 2)
                xT = score_ps[0]
                nc.scalar.copy(split[:, 3, :], xT).then_inc(s_split, 1)
                nc.scalar.activation(wx[:, :], xT, ACT.Copy, scale=w_c[:, 0:1]).then_inc(s_split, 1)
                act.wait_ge(s_split, 5 * b + 2)
                nc.scalar.copy(split[:, 0, :], wx[:, :]).then_inc(s_split, 1)
                act.wait_ge(s_rest, 2 * b + 1)
                nc.scalar.copy(split[:, 4, :], rest_k[:, :]).then_inc(s_split, 1)
                act.wait_ge(s_rest, 2 * b + 2)
                nc.scalar.copy(split[:, 1, :], rest_q[:, :]).then_inc(s_split, 1)
            with act.Fori(0, GROUPS) as g:
                for n in range(TILES * HG):
                    jt, h = n // HG, n % HG
                    act.wait_ge(s_S, 32 * g + n + 1)
                    nc.scalar.activation(E[:, jt % 2, h, :], score_ps[n % 2], ACT.Exp).then_inc(s_E, 1)

        @block.tensor
        def _(pe):
            pe.wait_ge(s_const, 6)
            with pe.Fori(0, B) as b:
                pe.wait_ge(s_norm, b + 1)
                for t in range(TILES):
                    last = nc.tensor.transpose(score_ps[0][:, P * t:P * (t + 1)], normed[:, t, :], ident[:, :])
                last.then_inc(s_xt, 1)
                pe.wait_ge(s_bin, b + 1)
                for half in range(2):
                    last = nc.tensor.matmul(score_ps[1][0:H, HALF * half:HALF * (half + 1)], signed_head[:, :],
                                            bound_in[:, HALF * half:HALF * (half + 1)], start=True, stop=True)
                last.then_inc(s_bmm, 1)
            pe.wait_ge(s_bound, 1)
            nc.tensor.transpose(aux_ps[0:1, 0:H], call[:, :], ident[0:H, 0:H]).then_inc(s_flag_t, 1)
            pe.wait_ge(s_flag, 1)
            general = pe.value_load(flag[0:1, 0:1], min_val=0, max_val=1)

            def score(k, jt, h, ps, left, right, rows):
                r = h % 2
                for half in range(2):
                    last = nc.tensor.matmul(
                        ps[:, HALF * half:HALF * (half + 1)],
                        left[k][64 * r:64 * r + rows, h // 2, P * jt:P * (jt + 1)],
                        right[k][64 * r:64 * r + rows, h // 2, HALF * half:HALF * (half + 1)],
                        start=True, stop=True, tile_position=(64 * r, 0))
                return last

            with pe.If(general == 1):
                with pe.Fori(0, GROUPS) as g:
                    pe.wait_ge(m_load, LOADED * (g + 1))
                    for n in range(HG * TILES):
                        h, it = n // TILES, n % TILES
                        pe.wait_ge(m_max, 32 * g + n + 1)
                        score(0, it, h, score_ps[n % 2], QT, KT, ROWS).then_inc(m_S, 1)
                    pe.wait_ge(m_max, 32 * g + 34)
                    nc.tensor.transpose(aux_ps[0:HG * TILES, 0:P], rmax[:, :, :].rearrange("p h t -> p (h t)"),
                                        ident[:, :]).then_inc(m_t, 1)

            def unit(k, n):
                score(k, n // HG, n % HG, score_ps[n % 2], KT, QT, SROWS).then_inc(s_S, 1)

            def pv(k, jt, half):
                for h in range(HG):
                    last = nc.tensor.matmul(
                        o_ps[VW * h:VW * (h + 1), HALF * half:HALF * (half + 1)], V[k][:, jt, h, :],
                        E[:, jt % 2, h, HALF * half:HALF * (half + 1)],
                        start=(jt == 0), stop=(jt == TILES - 1), tile_position=(0, VW * h))
                last.then_inc(s_pv, 1)

            def ffn_transpose(chunk):
                pe.wait_ge(s_fn, chunk + 1)
                for t in range(FT):
                    last = nc.tensor.transpose(aux_ps[:, P * t:P * (t + 1)], fn[:, t, :], ident[:, :])
                last.then_inc(s_fT, 1)

            def ffn_hidden(chunk, c):
                if c == 0:
                    pe.wait_ge(s_fTc, chunk + 1)
                last = nc.tensor.matmul(aux_ps[:, FT * P * c:FT * P * (c + 1)], W1[:, P * c:P * (c + 1)],
                                        fT[:, :], start=True, stop=True)
                if c == HC - 1:
                    last.then_inc(s_fc, 1)

            def ffn_project(chunk, t):
                if t == 0:
                    pe.wait_ge(s_relu2, chunk + 1)
                for c in range(HC):
                    last = nc.tensor.matmul(aux_ps[:, P * t:P * (t + 1)], relu2[:, c, P * t:P * (t + 1)],
                                            W2[:, c, :], start=(c == 0), stop=(c == HC - 1))
                if t == FT - 1:
                    last.then_inc(s_fp, 1)

            def group(s, k, ffn, last_group=False):
                g = 2 * s + k
                chunk = g - LAG
                for jt in range(TILES):
                    if jt == 0:
                        pe.wait_ge(s_v[k], s + (1 if k == 0 else 3))
                        pe.wait_ge(s_ev, 2 * g + 2)
                    for half in range(2):
                        n = HG * (jt + 1) + 2 * half
                        pv(k, jt, half)
                        for m in (n + 2, n + 3):
                            if m < 32:
                                pe.wait_ge(s_E, 32 * g + m - 1)
                                unit(k, m)
                            elif not last_group:
                                if m == 32:
                                    pe.wait_ge(s_qk[1 - k], LOADED * (s + 1 + k))
                                pe.wait_ge(s_E, 32 * g + m - 1)
                                unit(1 - k, m - 32)
                            elif half == 1 or m > 32:
                                pe.wait_ge(s_E, 32 * g + 32)
                        if ffn:
                            if (jt, half) == (1, 0):
                                pe.wait_ge(s_att, g + 1)
                                ffn_transpose(chunk)
                            if jt in (2, 3):
                                ffn_hidden(chunk, 2 * (jt - 2) + half)
                            if jt == 5:
                                ffn_project(chunk, half)
                if ffn:
                    pe.wait_ge(s_y, chunk + 1)
                else:
                    pe.wait_ge(s_att, g + 1)
                for t in range(TILES):
                    if t % 4 == 0:
                        pe.wait_ge(s_ev, 2 * g + 3 + t // 4)
                    last = nc.tensor.transpose(aux_ps[:, P * t:P * (t + 1)], o_sb[:, P * t:P * (t + 1)], ident[:, :])
                last.then_inc(s_to, 1)

            pe.wait_ge(s_qk[0], LOADED)
            for n in range(6):
                if n >= 2:
                    pe.wait_ge(s_E, n - 1)
                unit(0, n)
            with pe.Fori(0, 2) as s:
                for k in range(2):
                    group(s, k, False)
            pe.wait_ge(s_wd, 1)
            pe.wait_ge(s_att, 1 + LAG)
            for c in range(HC):
                nc.tensor.transpose(aux_ps[:, P * c:P * (c + 1)], wfc[:, c, :], ident[:, :])
            for c in range(HC):
                last = nc.tensor.transpose(aux_ps[:, HALF + P * c:HALF + P * (c + 1)], wpj[:, P * c:P * (c + 1)], ident[:, :])
            last.then_inc(s_wt, 1)
            pe.wait_ge(s_wd, 2)
            nc.tensor.transpose(aux_ps[0:RANK, 0:RANK], fb_sb[:, :], ident[0:RANK, 0:RANK])
            for c in range(HC):
                last = nc.tensor.transpose(aux_ps[0:RANK, HALF + P * c:HALF + P * (c + 1)], u_sb[:, c, :], ident[:, :])
            last.then_inc(s_wt, 1)
            pe.wait_ge(s_wd, 3)
            nc.tensor.matmul(aux_ps[0:RANK, 0:C], fbT[:, :], v_sb[:, :], start=True, stop=True).then_inc(s_wt, 1)
            pe.wait_ge(s_wd, 4)
            nc.tensor.matmul(aux_ps[:, 0:HID], fbv[:, :], uT[:, :], start=True, stop=True).then_inc(s_wt, 1)
            pe.wait_ge(s_wd, 5)
            with pe.Fori(2, STEPS - 1) as s:
                for k in range(2):
                    group(s, k, True)
            group(STEPS - 1, 0, True)
            group(STEPS - 1, 1, True, last_group=True)
            pe.wait_ge(s_att, GROUPS + 1)
            with pe.Fori(GROUPS - LAG, GROUPS) as chunk:
                pe.wait_ge(s_y, chunk)
                ffn_transpose(chunk)
                for c in range(HC):
                    ffn_hidden(chunk, c)
                for t in range(FT):
                    ffn_project(chunk, t)

        class Chain:

            def __init__(self, dve, done, before=0):
                self.dve, self.done, self.before, self.n = dve, done, before, 0

            def then(self, ins):
                ins.then_inc(self.done, 1)
                self.n += 1

            def ready(self):
                self.dve.wait_ge(self.done, self.before + self.n)

            def link(self, ins):
                self.then(ins)
                self.ready()

        def layernorm_rstd(dve, ch, mvs, v, r, t):
            ch.link(nc.vector.tensor_scalar(v, mvs[:, :, 1:2].rearrange("p t o -> p (t o)"), EPS, None, ALU.add))
            ch.link(nc.vector.tensor_scalar(t.bitcast(I32), v.bitcast(I32), 1, None, ALU.logical_shift_right))
            ch.link(nc.vector.tensor_scalar(r.bitcast(I32), t.bitcast(I32), -1.0, MAGIC, ALU.mult, ALU.add))
            for _ in range(3):
                ch.link(nc.vector.scalar_tensor_tensor(out=t, in0=r, scalar=-0.5, in1=r, op0=ALU.mult, op1=ALU.mult))
                ch.link(nc.vector.tensor_tensor(out=t, in0=t, in1=v, op=ALU.mult))
                ch.link(nc.vector.scalar_tensor_tensor(out=r, in0=t, scalar=1.5, in1=r, op0=ALU.add, op1=ALU.mult))

        RSQRT_LINKS = 12

        @block.vector
        def _(dve):
            ch = Chain(dve, c_pre)
            for i, (done, n) in enumerate(((s_xt, 1), (s_xn, 16), (s_parts, 16), (m_max, 2), (m_store, 64),
                                           (s_ev, 2), (s_out[0], 16), (s_out[1], 16))):
                nc.vector.memset(credit[:, i:i + 1], 0.0).then_inc(done, n)
            dve.wait_ge(s_wc, 32)
            ch.link(nc.vector.scalar_tensor_tensor(out=w_c[:, :], in0=rot_c[:, :], scalar=float(D) ** -0.5,
                                                   in1=ent_c[:, :], op0=ALU.mult, op1=ALU.mult))
            ch.then(nc.vector.tensor_scalar(sgn_c[:, :], w_c[:, :], 0.0, None, ALU.is_gt))
            ch.link(nc.vector.tensor_scalar(neg_c[:, :], w_c[:, :], 0.0, None, ALU.is_lt))
            ch.link(nc.vector.tensor_tensor(out=sgn_c[:, :], in0=sgn_c[:, :], in1=neg_c[:, :], op=ALU.subtract))
            dve.wait_ge(s_const, 6)
            ch.then(nc.vector.tensor_scalar(signed_head[:, :], head_of[:, :], sgn_c[:, 0:1], None, ALU.mult))
            for b in range(B):
                dve.wait_ge(s_x[b], 16)
                for t in range(TILES * b, TILES * (b + 1)):
                    ch.then(nc.vector.bn_stats(bn[:, t, :], X[:, t, :]))
                ch.ready()
                for t in range(TILES * b, TILES * (b + 1)):
                    ch.then(nc.vector.bn_aggr(mv[:, t, :], bn[:, t, :]))
            ch.ready()
            layernorm_rstd(dve, ch, mv, var[:, :], rstd[:, :], nt[:, :])
            with dve.Fori(0, B) as b:
                dve.wait_ge(s_xn, 16 * b + 16)
                dve.wait_ge(s_xt, b + 1)
                for t in range(TILES):
                    last = nc.vector.tensor_scalar(
                        normed[:, t, :], X[:, bass.ds(TILES * b + t, 1), :].rearrange("p t c -> p (t c)"),
                        mv[:, bass.ds(TILES * b + t, 1), 0:1].rearrange("p t o -> p (t o)"),
                        rstd[:, bass.ds(TILES * b + t, 1)], ALU.subtract, ALU.mult)
                last.then_inc(s_norm, 1)
                dve.wait_ge(s_split, 5 * b + 2)
                nc.vector.tensor_tensor(out=rest_k[:, :], in0=score_ps[0], in1=split[:, 3, :],
                                        op=ALU.subtract).then_inc(s_rest, 1)
                dve.wait_ge(s_split, 5 * b + 3)
                nc.vector.tensor_tensor(out=rest_q[:, :], in0=wx[:, :], in1=split[:, 0, :],
                                        op=ALU.subtract).then_inc(s_rest, 1)
                dve.wait_ge(s_split, 5 * b + 4)
                nc.vector.tensor_tensor(out=split[:, 5, :], in0=rest_k[:, :], in1=split[:, 4, :],
                                        op=ALU.subtract).then_inc(s_klow, 1)
                dve.wait_ge(s_bmm, b + 1)
                ch.then(nc.vector.tensor_reduce(cmax[:, bass.ds(b, 1)], score_ps[1][0:H, :], AX_X, ALU.max))
            ch.n += B - 1
            ch.ready()
            ch.then(nc.vector.tensor_scalar(cneg[:, :], cmax[:, :], -1.01, -1e-3, ALU.mult, ALU.add))
            nc.vector.tensor_reduce(call[:, :], cmax[:, :], AX_X, ALU.max).then_inc(s_bound, 1)
            ch.ready()
            dve.wait_ge(s_preset, 1)
            for b in range(B):
                last = nc.vector.tensor_scalar(shift_rows[:, b, 0, :], zrow[:, :], cneg[:, b:b + 1], None, ALU.add)
            last.then_inc(s_shr, 1)
            dve.wait_ge(s_flag_t, 1)
            nc.vector.tensor_reduce(call1[:, :], aux_ps[0:1, 0:H], AX_X, ALU.max).then_inc(s_att, 1)
            dve.wait_ge(s_att, 1)
            nc.vector.tensor_scalar(flag[:, :], call1[:, :], SHIFT_LIMIT, None, ALU.is_gt).then_inc(s_flag, 1)
            dve.wait_ge(s_flag, 1)
            general = dve.value_load(flag[0:1, 0:1], min_val=0, max_val=1)
            with dve.If(general == 1):
                with dve.Fori(0, GROUPS) as g:
                    for n in range(HG * TILES):
                        dve.wait_ge(m_S, 32 * g + n + 1)
                        nc.vector.tensor_reduce(rmax[:, n // TILES, n % TILES:n % TILES + 1], score_ps[n % 2],
                                                AX_X, ALU.max).then_inc(m_max, 1)
                    gc = Chain(dve, c_general, 5 * g)
                    dve.wait_ge(m_t, g + 1)
                    gc.link(nc.vector.tensor_scalar(nmax[:, :], aux_ps[0:HG * TILES, 0:P], -1.0, None, ALU.mult))
                    gc.link(nc.vector.tensor_copy(nparts[:, 0, :], nmax[:, :]))
                    gc.link(nc.vector.tensor_tensor(out=nres[:, :], in0=nmax[:, :], in1=nparts[:, 0, :], op=ALU.subtract))
                    gc.link(nc.vector.tensor_copy(nparts[:, 1, :], nres[:, :]))
                    gc.link(nc.vector.tensor_tensor(out=nmax[:, :], in0=nres[:, :], in1=nparts[:, 1, :], op=ALU.subtract))
                    nc.vector.tensor_copy(nparts[:, 2, :], nmax[:, :]).then_inc(m_parts, 1)

            wc = Chain(dve, c_weights)
            dve.wait_ge(s_w, 16 * 6)

            def ternary(w, rows, width):
                a = wa[:, :].rearrange("p (t c) -> p t c", t=rows)
                m = wb[:, :].rearrange("p (t c) -> p t c", t=rows)

                def wide(x):
                    return x[:, 0:rows].rearrange("p (t o) -> p t o", o=1).to_broadcast([P, rows, width])

                wc.link(nc.vector.tensor_reduce(ws[:, 0:rows], w, AX_X, ALU.add, apply_absolute_value=True))
                wc.link(nc.vector.tensor_scalar(ws[:, 0:rows], ws[:, 0:rows], 1.0 / width, EPS, ALU.mult, ALU.max))
                wc.then(nc.vector.tensor_scalar(wh[:, 0:rows], ws[:, 0:rows], 0.5, None, ALU.mult))
                wc.link(nc.vector.tensor_scalar(wnh[:, 0:rows], ws[:, 0:rows], -0.5, None, ALU.mult))
                wc.then(nc.vector.tensor_tensor(out=a, in0=w, in1=wide(wh), op=ALU.is_gt))
                wc.link(nc.vector.tensor_tensor(out=m, in0=w, in1=wide(wnh), op=ALU.is_lt))
                wc.link(nc.vector.tensor_tensor(out=a, in0=a, in1=m, op=ALU.subtract))
                wc.link(nc.vector.tensor_tensor(out=m, in0=a, in1=w, op=ALU.subtract))
                wc.link(nc.vector.tensor_tensor(out=a, in0=m, in1=w, op=ALU.add))
                wc.link(nc.vector.tensor_tensor(out=w, in0=a, in1=wide(ws), op=ALU.mult))

            ternary(wfc[:, :, :], HC, C)
            ternary(wpj[:, :].rearrange("p (t c) -> p t c", t=1), 1, HID)
            nc.vector.memset(wh[:, :], 0.0).then_inc(s_wd, 1)

            def finish_group(chain, s, k):
                g = 2 * s + k
                for half in range(2):
                    dve.wait_ge(s_pv, 16 * g + 15 + half)
                    nc.vector.tensor_copy(o_sb[:, HALF * half:HALF * (half + 1)],
                                          o_ps[:, HALF * half:HALF * (half + 1)]).then_inc(s_ev, 1)
                dve.wait_ge(s_to, g + 1)
                heads = aux_ps.rearrange("p (t h v) -> p t h v", t=TILES, h=HG)
                chain.link(nc.vector.reciprocal(rden[:, :, :], heads[:, :, :, D:D + 1].rearrange("p t h o -> p t (h o)")))
                nc.vector.tensor_tensor(
                    out=att[:, :, :, :].rearrange("p t h d -> p (t h) d"),
                    in0=aux_ps.rearrange("p (th v) -> p th v", v=VW)[:, :, 0:D],
                    in1=rden[:, :, :].rearrange("p t (h o) -> p (t h) o", o=1).to_broadcast([P, TILES * HG, D]),
                    op=ALU.mult).then_inc(s_att, 1)
                dve.wait_ge(s_att, g + 2)
                xs = X[:, bass.ds(TILES * (s // 2), TILES), bass.ds(64 * (s % 2) + 32 * k, HG * D)]
                chain.link(nc.vector.tensor_tensor(out=xs, in0=xs, in1=att[:, :, :, :].rearrange("p t h d -> p t (h d)"),
                                                   op=ALU.add))

            FINISH_LINKS = 2

            def ffn(chain, pair, k):
                chunk = 2 * pair + k

                def tile(t):
                    return X[:, bass.ds(FT * chunk + t, 1), :].rearrange("p t c -> p (t c)")

                for t in range(FT):
                    chain.then(nc.vector.bn_stats(fbn[:, t, :], tile(t)))
                chain.ready()
                chain.then(nc.vector.memset(fnt[:, :], 0.0))
                for t in range(FT):
                    chain.then(nc.vector.bn_aggr(fmv[:, t, :], fbn[:, t, :]))
                chain.ready()
                layernorm_rstd(dve, chain, fmv, fvar[:, :], frstd[:, :], fnt[:, :])
                for t in range(FT):
                    last = nc.vector.tensor_scalar(fn[:, t, :], tile(t), fmv[:, t, 0:1], frstd[:, t:t + 1],
                                                   ALU.subtract, ALU.mult)
                last.then_inc(s_fn, 1)
                dve.wait_ge(s_fT, chunk + 1)
                nc.vector.tensor_copy(fT[:, :], aux_ps[:, 0:FT * P]).then_inc(s_fTc, 1)
                dve.wait_ge(s_fc, chunk + 1)
                nc.vector.tensor_scalar(relu[:, :, :].rearrange("p c n -> p (c n)"), aux_ps, 0.0, None,
                                        ALU.max).then_inc(s_relu, 1)
                dve.wait_ge(s_fp, chunk + 1)
                dve.wait_ge(s_out[k], 16 * pair + 16)
                nc.vector.tensor_tensor(
                    out=y[k][:, :, :], in0=aux_ps[:, 0:FT * P].rearrange("p (t c) -> p t c", c=C),
                    in1=X[:, bass.ds(FT * chunk, FT), :], op=ALU.add).then_inc(s_y, 1)

            FFN_LINKS = 2 * FT + RSQRT_LINKS + 1

            with dve.Fori(0, 2) as s:
                for k in range(2):
                    finish_group(Chain(dve, c_first, FINISH_LINKS * (2 * s + k)), s, k)
            dve.wait_ge(s_wt, 1)
            nc.vector.tensor_copy(W1[:, :], aux_ps[:, 0:HID])
            nc.vector.tensor_copy(W2[:, :, :], aux_ps[:, HALF:2 * HALF].rearrange("p (t c) -> p t c", c=C)).then_inc(s_wd, 1)
            dve.wait_ge(s_wt, 2)
            nc.vector.tensor_copy(fbT[:, :], aux_ps[0:RANK, 0:RANK])
            nc.vector.tensor_copy(uT[:, :], aux_ps[0:RANK, HALF:2 * HALF]).then_inc(s_wd, 1)
            dve.wait_ge(s_wt, 3)
            nc.vector.tensor_scalar(fbv[:, :], aux_ps[0:RANK, 0:C], gate_c[:, 0:1], None, ALU.mult).then_inc(s_wd, 1)
            dve.wait_ge(s_wt, 4)
            nc.vector.tensor_tensor(out=W1[:, :], in0=aux_ps[:, 0:HID], in1=W1[:, :], op=ALU.add).then_inc(s_wd, 1)
            each = FINISH_LINKS + FFN_LINKS
            with dve.Fori(2, STEPS - 1) as s:
                for k in range(2):
                    chain = Chain(dve, c_mid, each * (2 * s + k - LAG))
                    ffn(chain, s - LAG // 2, k)
                    finish_group(chain, s, k)
                    assert chain.n == each
            chain = Chain(dve, c_last)
            for k in range(2):
                ffn(chain, STEPS - 1 - LAG // 2, k)
                finish_group(chain, STEPS - 1, k)
            with dve.Fori(0, LAG // 2) as i:
                for k in range(2):
                    ffn(Chain(dve, c_tail, FFN_LINKS * (2 * i + k)), STEPS - LAG // 2 + i, k)


_INS = ["L0_attn_inputs", "L0_attn_rotation_params", "L0_attn_entangle_params", "L0_ffn_fast_b",
        "L0_ffn_w_fc", "L0_ffn_w_proj", "L0_ffn_u", "L0_ffn_v", "L0_ffn_gate"]


def kernel(**inputs):
    import numpy as _np
    import concourse.bacc as _bacc
    from concourse import mybir as _mybir
    from concourse.bass_utils import run_bass_kernel_spmd as _run

    nc = _bacc.Bacc("TRN2", target_bir_lowering=False, num_devices=1)
    arrays, args = {}, []
    for name in _INS:
        a = _np.ascontiguousarray(inputs[name])
        a = a.reshape(1) if a.ndim == 0 else a
        arrays[f"in_{name}_dram"] = a
        args.append(nc.dram_tensor(f"in_{name}_dram", a.shape, _mybir.dt.from_np(a.dtype), kind="ExternalInput").ap())
    args.append(nc.dram_tensor("out_0_dram", (B, T, C), _mybir.dt.float32, kind="ExternalOutput").ap())
    build(nc, *args)
    r = _run(nc, [arrays], core_ids=[0])
    return r.results[0]["out_0_dram"]
```

```python
from contextlib import ExitStack

import concourse.bass as bass
from concourse import mybir

F32, BF16, I32 = mybir.dt.float32, mybir.dt.bfloat16, mybir.dt.int32
ACT = mybir.ActivationFunctionType
ALU = mybir.AluOpType
AX_X = mybir.AxisListType.X

B, T, C, H = 4, 1024, 128, 16
D = C // H
P = 128
TILES = T // P
HG = 4
GROUPS = B * H // HG
STEPS = GROUPS // 2
HALF = 512
PARTS = 6
ROWS = 6 * D
SROWS = ROWS + 3
VW = 32
HID, RANK = 512, 16
HC = HID // P
FT = 2
EPS = 1e-5
SHIFT_LIMIT = 40.0
MAGIC = float(0x5F3759DF)
WARM_UP = 24
SPLIT_TILES = 6
ST = SPLIT_TILES * P
BOUNDS = 1 + B * H
TAIL = TILES // 2
LAG = 4


def build(nc, x_in, rot, ent, fast_b, w_fc, w_proj, u_in, v_in, gate, out):
    q_dram = nc.dram_tensor("q_scratch", (C, 6, B * T), BF16, kind="Internal").ap()
    k_dram = nc.dram_tensor("k_scratch", (C, 6, B * T), BF16, kind="Internal").ap()
    shift_dram = nc.dram_tensor("shift_scratch", (B * H, 3, T), BF16, kind="Internal").ap()

    with ExitStack() as ctx:
        def sb(name, shape, dt=F32):
            return ctx.enter_context(nc.sbuf_tensor(name, shape, dt))

        def sem(name):
            return ctx.enter_context(nc.semaphore(name))

        psum = ctx.enter_context(nc.psum_tensor("psum", [P, 4096], F32))
        score_ps = [psum[:, 0:1024], psum[:, 1024:2048]]
        o_ps = psum[:, 2048:3072]
        aux_ps = psum[:, 3072:4096]

        X = sb("X", [P, B * TILES, C])
        XN = sb("XN", [P, B * TILES, C])
        staged = sb("staged", [P, SPLIT_TILES, C])
        split = sb("split", [P, PARTS, T], BF16)
        wx, rest_k, rest_q = (sb(n, [P, T]) for n in ("wx", "rest_k", "rest_q"))
        later = sb("later_split", [P, PARTS, ST], BF16)
        later_wx, later_k, later_q = (sb(n, [P, ST]) for n in ("later_wx", "later_rest_k", "later_rest_q"))
        bounds = sb("bounds", [P, BOUNDS])
        by_tile = sb("bounds_by_tile", [P, TILES, H])
        shift_rows = sb("shift_rows", [BOUNDS, 3, T], BF16)
        QT = [sb(f"QT{k}", [P, 2, T], BF16) for k in range(2)]
        KT = [sb(f"KT{k}", [P, 2, T], BF16) for k in range(2)]
        V = [sb(f"V{k}", [P, TILES, HG, VW]) for k in range(2)]
        E = sb("E", [P, 2, HG, T])
        o_sb = sb("o_sb", [P, T])
        att = sb("att", [P, TILES, HG, D])
        rden = sb("rden", [P, TILES, HG])
        bn = sb("bn", [P, B * TILES, 6])
        mv = sb("mv", [P, B * TILES, 2])
        var = sb("var", [P, B * TILES])
        rstd = sb("rstd", [P, B * TILES])
        nt = sb("nt", [P, B * TILES])
        nmr = sb("neg_mean_over_deviation", [P, B * TILES])
        fbn, fmv = sb("fbn", [P, FT, 6]), sb("fmv", [P, FT, 2])
        fvar, frstd, fnt = sb("fvar", [P, FT]), sb("frstd", [P, FT]), sb("fnt", [P, FT])
        fn = sb("fn", [P, FT, C])
        fT = sb("fT", [P, FT * P])
        relu = sb("relu", [P, HC, FT * P])
        relu2 = sb("relu2", [P, HC, FT * P])
        y = [sb(f"y{k}", [P, FT, C]) for k in range(2)]
        ident = sb("ident", [P, P])
        rot_c, ent_c, w_c = (sb(n, [P, 1]) for n in ("rot_c", "ent_c", "w_c"))
        rot_r, ent_r, w_r, wabs = (sb(n, [P, C]) for n in ("rot_r", "ent_r", "w_r", "w_abs"))
        credit = sb("credit", [P, 16])
        bmax = sb("bmax", [BOUNDS, 1])
        bneg = sb("bneg", [BOUNDS, 1])
        flag = sb("flag", [1, 1], I32)
        zrow = sb("zrow", [BOUNDS, T], BF16)
        weights = sb("weights", [P, 2, HID])
        wfc = weights[:, 0, :].rearrange("p (c n) -> p c n", c=HC)
        wpj = weights[:, 1, :]
        staged_w = sb("staged_weights", [P, HID])
        weights_T = sb("weights_T", [P, 2, HID])
        W1 = weights_T[:, 0, :]
        W2 = weights_T[:, 1, :].rearrange("p (c n) -> p c n", c=HC)
        wa, wb = sb("wa", [P, 512]), sb("wb", [P, 512])
        ws, wh = sb("ws", [P, HC]), sb("wh", [P, HC])
        wnh = sb("wnh", [P, HC])
        u_sb = sb("u_sb", [P, HC, RANK])
        v_sb = sb("v_sb", [RANK, C])
        fb_sb = sb("fb_sb", [RANK, RANK])
        fbT = sb("fbT", [RANK, RANK])
        fbv = sb("fbv", [RANK, C])
        uT = sb("uT", [RANK, HID])
        gate_c = sb("gate_c", [RANK, 1])
        low_rank = sb("low_rank", [P, HID])
        rmax = sb("rmax", [P, HG, TILES])
        nmax = sb("nmax", [HG * TILES, P])
        nres = sb("nres", [HG * TILES, P])
        nparts = sb("nparts", [HG * TILES, 3, P], BF16)

        s_x = [sem(f"s_x{b}") for b in range(B)]
        s_w = sem("s_weights_loaded")
        s_lw = sem("s_low_rank_weights_loaded")
        s_wc = sem("s_rot_ent_loaded")
        s_const = sem("s_constants")
        s_preset = sem("s_operands_preset")
        s_norm = sem("s_normed")
        s_xt = sem("s_x_transposed")
        s_split = sem("s_act_split")
        s_rest_k = sem("s_rest_k")
        s_rest_q = sem("s_rest_q")
        s_klow = sem("s_k_low_part")
        s_qlow = sem("s_q_low_part")
        s_parts = sem("s_parts_stored")
        s_stat = sem("s_statistics")
        s_sq = sem("s_squares")
        s_wsq = sem("s_weighted_squares")
        s_bt = sem("s_bounds_by_token")
        s_btt = sem("s_bounds_transposed")
        s_shr = sem("s_shift_rows")
        s_shift = sem("s_shift_stored")
        s_flag = sem("s_flag")
        s_lt = sem("s_low_rank_product")
        s_lr = sem("s_low_rank_copied")
        later_sems = [[sem(f"{m}_later_{n}") for n in ("staged", "transposed", "read", "split", "stored")]
                      for m in "sm"]
        s_qk = [sem(f"s_qk{k}") for k in range(2)]
        s_v = [sem(f"s_v{k}") for k in range(2)]
        s_S = sem("s_scores")
        s_E = sem("s_exps")
        s_pv = sem("s_pv")
        s_ev = sem("s_o_evacuated")
        s_to = sem("s_o_transposed")
        s_att = sem("s_attention_read")
        s_tail = sem("s_tail_products")
        s_tail_n = sem("s_tail_normed")
        s_tail_c = sem("s_tail_copied")
        s_tail_r = sem("s_tail_relu")
        s_tail_r2 = [sem(f"s_tail_relu2_{n}") for n in ("vector", "gpsimd")]
        s_tail_out = [sem(f"s_tail_out_stored{f}") for f in range(2)]
        s_wabs = sem("s_w_abs")
        s_tail_y = sem("s_tail_y")
        s_fTc = sem("s_ffn_transposed_copied")
        s_fn = sem("s_ffn_normed")
        s_fT = sem("s_ffn_transposed")
        s_fc = sem("s_ffn_hidden")
        s_relu = sem("s_ffn_relu")
        s_relu2 = sem("s_ffn_relu2")
        s_fp = sem("s_ffn_projected")
        s_y = sem("s_y")
        s_out = [sem(f"s_out_stored{k}") for k in range(2)]
        s_ws = sem("s_weights_staged")
        s_wt = sem("s_weights_transposed")
        s_wd = sem("s_weights_copied")
        c_pre, c_split, c_general, c_first, c_mid, c_weights, c_last, c_tail = (
            sem(f"c_{n}") for n in ("pre", "split", "general", "first", "mid", "weights", "last", "tail"))
        m_load = sem("m_operands_loaded")
        m_S = sem("m_scores")
        m_max = sem("m_max")
        m_t = sem("m_max_transposed")
        m_parts = sem("m_max_parts")
        m_store = sem("m_shift_stored")

        def load_parts(sp, group, k, done):
            for r in range(2):
                for dst, src in ((QT[k], q_dram), (KT[k], k_dram)):
                    heads = src.rearrange("(x r d) t n -> r x d t n", r=2, d=D)[r]
                    sp.dma_start(dst[64 * r:64 * r + ROWS, :, :],
                                 heads[bass.ds(2 * (group % 4), 2), :, :, bass.ds(T * (group // 4), T)]
                                 .rearrange("x d t n -> (d t) x n")).then_inc(done, 16)

        def load_shifts(sp, group, k, done):
            for r in range(2):
                rows = 64 * r + ROWS
                sp.dma_start(QT[k][rows:rows + 3, :, :],
                             shift_dram.rearrange("(x r) p n -> r p x n", r=2)[r, :, bass.ds(2 * group, 2), :]).then_inc(done, 16)

        PARTS_LOADED = 4 * 16
        LOADED = 6 * 16

        def out_rows(chunk):
            return out.rearrange("b t c -> (b t) c")[bass.ds(chunk * (FT * P), FT * P), :].rearrange("(t p) c -> p t c", p=P)

        def store_parts(sp, parts, tokens, done):
            q, x, n = parts[:, 0:3, :], parts[:, 3:6, :], parts.shape[2]
            sp.dma_start(k_dram[:, 0:3, tokens], x[:, 0:1, :].to_broadcast([P, 3, n])).then_inc(done, 16)
            sp.dma_start(k_dram[:, 3:5, tokens], x[:, 1:2, :].to_broadcast([P, 2, n])).then_inc(done, 16)
            sp.dma_start(k_dram[:, 5:6, tokens], x[:, 2:3, :]).then_inc(done, 16)
            sp.dma_start(q_dram[:, 0:3, tokens], q).then_inc(done, 16)
            sp.dma_start(q_dram[:, 3:5, tokens], q[:, 0:2, :]).then_inc(done, 16)
            sp.dma_start(q_dram[:, 5:6, tokens], q[:, 0:1, :]).then_inc(done, 16)

        def stage_later(pool, i, sems):
            is_staged, transposed = sems[0], sems[1]
            pool.wait_ge(transposed, i + 1)
            nc.gpsimd.tensor_copy(staged[:, :, :], XN[:, bass.ds(TILES + SPLIT_TILES * i, SPLIT_TILES), :]).then_inc(is_staged, 1)

        def transpose_later(pe, i, sems):
            is_staged, transposed = sems[0], sems[1]
            pe.wait_ge(is_staged, i + 1)
            for t in range(SPLIT_TILES):
                last = nc.tensor.transpose(aux_ps[:, P * t:P * (t + 1)], staged[:, t, :], ident[:, :])
            last.then_inc(transposed, 1)

        def split_later(dve, chain, i, sems):
            _, transposed, read, is_split, stored = sems
            x = aux_ps[:, 0:ST]
            dve.wait_ge(stored, 16 * PARTS * i + 16)
            dve.wait_ge(transposed, i + 2)
            chain.then(nc.vector.tensor_copy(later[:, 3, :], x))
            chain.link(nc.vector.tensor_scalar(later_wx[:, :], x, w_c[:, 0:1], None, ALU.mult))
            nc.vector.tensor_tensor(out=later_k[:, :], in0=x, in1=later[:, 3, :], op=ALU.subtract).then_inc(read, 1)
            chain.link(nc.vector.tensor_copy(later[:, 0, :], later_wx[:, :]))
            chain.then(nc.vector.tensor_tensor(out=later_q[:, :], in0=later_wx[:, :], in1=later[:, 0, :], op=ALU.subtract))
            dve.wait_ge(read, i + 2)
            chain.link(nc.vector.tensor_copy(later[:, 4, :], later_k[:, :]))
            chain.then(nc.vector.tensor_copy(later[:, 1, :], later_q[:, :]))
            chain.link(nc.vector.tensor_tensor(out=later[:, 5, :], in0=later_k[:, :], in1=later[:, 4, :], op=ALU.subtract))
            nc.vector.tensor_tensor(out=later[:, 2, :], in0=later_q[:, :], in1=later[:, 1, :],
                                    op=ALU.subtract).then_inc(is_split, 1)

        SPLIT_LINKS = 7

        def store_later(sp, i, sems):
            is_split, stored = sems[3], sems[4]
            sp.wait_ge(is_split, i + 1)
            store_parts(sp, later, bass.ds(T + ST * i, ST), stored)

        main_later, general_later = later_sems
        LATER = (B - 1) * TILES // SPLIT_TILES
        assert LATER == LAG

        block = ctx.enter_context(nc.Block())

        def squares(b):
            return E[:, 0, b, :].rearrange("p (t c) -> p t c", c=C)

        def weighted(b):
            return E[:, 1, b, :].rearrange("p (t c) -> p t c", c=C)

        tail_r = E[:, 0, :, :].rearrange("p h (u n) -> p (h u) n", n=HALF)
        tail_r2 = E[:, 1, :, :].rearrange("p h (u n) -> p (h u) n", n=HALF)
        tail_fn = XN[:, 0:TILES, :]
        tail_y = XN[:, TILES:2 * TILES, :]
        tail_fT = o_sb[:, :].rearrange("p (f n) -> p f n", f=2)

        def tail_t(f):
            return aux_ps[:, HALF * f:HALF * (f + 1)]

        def tail_h(f, c):
            return psum[:, 2048 * f + HALF * c:2048 * f + HALF * (c + 1)]

        def square_tail(engine, ops, n):
            engine.wait_ge(s_tail_r, n + 1)
            ops.tensor_tensor(out=tail_r2[:, n, :], in0=tail_r[:, n, :], in1=tail_r[:, n, :],
                              op=ALU.mult).then_inc(s_tail_r2[n % 2], 1)

        @block.sync
        def _(sp):
            for b in range(B):
                sp.dma_start(X[:, TILES * b:TILES * (b + 1), :],
                             x_in[b].rearrange("(t p) c -> p t c", p=P)).then_inc(s_x[b], 16)
                if b == 0:
                    sp.dma_start(rot_c[:, :], rot.rearrange("h (d o) -> (h d) o", o=1)).then_inc(s_wc, 16)
                    sp.dma_start(ent_c[:, :], ent.rearrange("h (d o) -> (h d) o", o=1)).then_inc(s_wc, 16)
                    for row, src in ((rot_r, rot), (ent_r, ent)):
                        sp.dma_start(row[:, :], src.rearrange("(a h) d -> a (h d)", a=1).to_broadcast([P, C])).then_inc(s_wc, 16)
                    sp.dma_start(u_sb[:, :, :], u_in.rearrange("(t p) r -> p t r", p=P)).then_inc(s_lw, 16)
                    sp.dma_start(v_sb[:, :], v_in).then_inc(s_lw, 16)
                    sp.dma_start(fb_sb[:, :], fast_b).then_inc(s_lw, 16)
                    sp.dma_start(gate_c[:, :], gate.rearrange("(a b) -> a b", a=1).to_broadcast([RANK, 1])).then_inc(s_lw, 16)
            sp.dma_start(wfc, w_fc.rearrange("(t p) c -> p t c", p=P)).then_inc(s_w, 16)
            sp.dma_start(wpj, w_proj).then_inc(s_w, 16)
            sp.wait_ge(s_split, 4)
            sp.wait_ge(s_klow, 1)
            sp.wait_ge(s_split, 5)
            sp.wait_ge(s_qlow, 1)
            store_parts(sp, split, slice(0, T), s_parts)
            sp.wait_ge(s_parts, 16 * PARTS)
            sp.wait_ge(s_preset, 1)
            for k in range(2):
                load_parts(sp, k, k, s_qk[k])
            sp.wait_ge(s_shr, 1)
            sp.dma_start(shift_dram, shift_rows[1:BOUNDS, :, :]).then_inc(s_shift, 16)
            sp.wait_ge(s_shift, 16)
            sp.wait_ge(s_flag, 1)
            general = sp.value_load(flag[0:1, 0:1], min_val=0, max_val=1)
            with sp.If(general == 1):
                with sp.Fori(0, LATER) as i:
                    store_later(sp, i, general_later)
                sp.wait_ge(general_later[4], 16 * PARTS * LATER + 16)
                with sp.Fori(0, GROUPS) as g:
                    sp.wait_ge(m_store, 16 * HG * g + 64)
                    load_parts(sp, g, 0, m_load)
                    sp.wait_ge(m_parts, g + 1)
                    for h in range(HG):
                        sp.dma_start(
                            shift_dram[bass.ds(HG * g + h, 1), :, :].rearrange("h p (t n) -> (h t) p n", n=P),
                            nparts[TILES * h:TILES * (h + 1), :, :]).then_inc(m_store, 16)
                sp.wait_ge(m_store, 16 * HG * GROUPS + 64)
                load_parts(sp, 0, 0, m_load)
            for k in range(2):
                load_shifts(sp, k, k, s_qk[k])

            def next_load(s, k):
                sp.wait_ge(s_S, 64 * s + 32 * k - 32)
                load_parts(sp, 2 * s + k, k, s_qk[k])
                load_shifts(sp, 2 * s + k, k, s_qk[k])

            def store(chunk, k):
                sp.wait_ge(s_y, chunk + 1)
                sp.dma_start(out_rows(chunk), y[k][:, :, :]).then_inc(s_out[k], 16)

            with sp.Fori(0, LATER // 2) as s:
                for k in range(2):
                    store_later(sp, 2 * s + k, main_later)
                    sp.wait_ge(main_later[4], 16 * PARTS * (2 * s + k) + 16 * PARTS + 16)
                    next_load(s + 1, k)
            with sp.Fori(3, STEPS) as s:
                for k in range(2):
                    next_load(s, k)
                    store(2 * s + k - 6, k)
            for k in range(2):
                store(2 * STEPS + k - 6, k)
            for f in range(2):
                sp.wait_ge(s_tail_y, f + 1)
                first = (B - 1) * TILES + TAIL * f
                sp.dma_start(out.rearrange("b t c -> (b t) c")[P * first:P * (first + TAIL), :]
                             .rearrange("(t p) c -> p t c", p=P), tail_y[:, TAIL * f:TAIL * (f + 1), :]).then_inc(s_tail_out[f], 16)
            for k in range(2):
                sp.wait_ge(s_out[k], 16 + 16 * (GROUPS - LAG) // 2)
                sp.wait_ge(s_tail_out[k], 16)

        @block.gpsimd
        def _(pool):
            nc.gpsimd.memset(ident[:, :], 0.0).then_inc(s_const, 1)
            pool.wait_ge(s_const, 1)
            nc.gpsimd.affine_select(out=ident[:, :], in_=ident[:, :], compare_op=ALU.not_equal, fill=1.0,
                                    base=0, pattern=[[-1, P]], channel_multiplier=1).then_inc(s_const, 1)
            for k in range(2):
                last = nc.gpsimd.memset(KT[k][:, :, :], 1.0)
            last.then_inc(s_preset, 1)
            nc.gpsimd.memset(zrow[:, :], 0.0)
            nc.gpsimd.memset(shift_rows[:, :, :], 0.0).then_inc(s_preset, 1)
            nc.gpsimd.memset(V[0][:, :, :, :], 0.0)
            nc.gpsimd.memset(V[1][:, :, :, :], 0.0).then_inc(s_v[1], 1)
            pool.wait_ge(s_v[1], 1)
            nc.gpsimd.memset(V[0][:, :, :, D:D + 1], 1.0)
            nc.gpsimd.memset(V[1][:, :, :, D:D + 1], 1.0).then_inc(s_v[1], 1)

            def weight_squares(b):
                pool.wait_ge(s_sq, b + 1)
                if b == 0:
                    pool.wait_ge(s_wabs, 1)
                nc.gpsimd.tensor_tensor(
                    out=weighted(b), in0=squares(b),
                    in1=wabs[:, :].rearrange("p (o c) -> p o c", o=1).to_broadcast([P, TILES, C]),
                    op=ALU.mult).then_inc(s_wsq, 1)

            pool.wait_ge(s_split, 3)
            nc.gpsimd.tensor_tensor(out=rest_q[:, :], in0=wx[:, :], in1=split[:, 0, :],
                                    op=ALU.subtract).then_inc(s_rest_q, 1)
            pool.wait_ge(s_split, 5)
            nc.gpsimd.tensor_tensor(out=split[:, 2, :], in0=rest_q[:, :], in1=split[:, 1, :],
                                    op=ALU.subtract).then_inc(s_qlow, 1)
            for b in range(B):
                weight_squares(b)
            pool.wait_ge(s_flag, 1)
            general = pool.value_load(flag[0:1, 0:1], min_val=0, max_val=1)
            with pool.If(general == 1):
                pool.wait_ge(s_norm, B)
                with pool.Fori(0, LATER) as i:
                    stage_later(pool, i, general_later)
                pool.wait_ge(general_later[1], LATER + 1)

            def values(step, k):
                nc.gpsimd.tensor_copy(
                    V[k][:, :, :, 0:D],
                    XN[:, bass.ds(TILES * (step // 2), TILES), bass.ds(64 * (step % 2) + 32 * k, HG * D)]
                    .rearrange("p t (h d) -> p t h d", d=D)).then_inc(s_v[k], 1)

            def square(chunk):
                pool.wait_ge(s_relu, chunk + 1)
                nc.gpsimd.tensor_tensor(out=relu2[:, :, :], in0=relu[:, :, :], in1=relu[:, :, :],
                                        op=ALU.mult).then_inc(s_relu2, 1)

            pool.wait_ge(s_norm, B)
            values(0, 0)
            values(0, 1)
            with pool.Fori(0, LATER // 2) as s:
                for k in range(2):
                    stage_later(pool, 2 * s + k, main_later)
                    if k == 1:
                        pool.wait_ge(s_wd, s + 1)
                        nc.gpsimd.tensor_copy(staged_w[:, :], weights[:, bass.ds(s, 1), :].rearrange("p o n -> p (o n)")).then_inc(s_ws, 1)
                    pool.wait_ge(s_pv, 32 * s + 16 * k + 16)
                    values(s + 1, k)
            with pool.Fori(2, STEPS - 1) as s:
                for k in range(2):
                    square(2 * s + k - LAG)
                    pool.wait_ge(s_pv, 32 * s + 16 * k + 16)
                    values(s + 1, k)
            for k in range(2):
                square(2 * STEPS - 2 + k - LAG)
            for c in range(1, 2 * HC, 2):
                square_tail(pool, nc.gpsimd, c)

        @block.scalar
        def _(act):
            act.wait_ge(s_lt, 1)
            nc.scalar.copy(fbT[:, :], o_ps[0:RANK, 0:RANK])
            nc.scalar.copy(uT[:, :], o_ps[0:RANK, HALF:2 * HALF]).then_inc(s_lr, 1)
            act.wait_ge(s_lt, 2)
            act.wait_ge(s_lw, 64)
            nc.scalar.activation(fbv[:, :], aux_ps[0:RANK, 0:C], ACT.Copy, scale=gate_c[:, 0:1]).then_inc(s_lr, 1)
            act.wait_ge(s_lt, 3)
            nc.scalar.copy(low_rank[:, :], o_ps[:, 0:HID]).then_inc(s_lr, 1)
            xT = score_ps[0]
            act.wait_ge(s_xt, 1)
            nc.scalar.copy(split[:, 3, :], xT).then_inc(s_split, 1)
            act.wait_ge(s_wabs, 1)
            nc.scalar.activation(wx[:, :], xT, ACT.Copy, scale=w_c[:, 0:1]).then_inc(s_split, 1)
            act.wait_ge(s_split, 2)
            nc.scalar.copy(split[:, 0, :], wx[:, :]).then_inc(s_split, 1)
            act.wait_ge(s_rest_k, 1)
            nc.scalar.copy(split[:, 4, :], rest_k[:, :]).then_inc(s_split, 1)
            act.wait_ge(s_rest_q, 1)
            nc.scalar.copy(split[:, 1, :], rest_q[:, :]).then_inc(s_split, 1)
            nc.scalar.activation(squares(0), XN[:, 0:TILES, :], ACT.Square).then_inc(s_sq, 1)
            act.wait_ge(s_stat, 1)
            for b in range(1, B):
                for t in range(TILES):
                    n = TILES * b + t
                    last = nc.scalar.activation(squares(b)[:, t, :], X[:, n, :], ACT.Square,
                                                bias=nmr[:, n:n + 1], scale=rstd[:, n:n + 1])
                last.then_inc(s_sq, 1)
            act.wait_ge(s_bt, 1)
            with act.Fori(0, GROUPS) as g:
                for n in range(TILES * HG):
                    jt, h = n // HG, n % HG
                    act.wait_ge(s_S, 32 * g + n + 1)
                    nc.scalar.activation(E[:, jt % 2, h, :], score_ps[n % 2], ACT.Exp).then_inc(s_E, 1)

            for f in range(2):
                act.wait_ge(s_tail, f + 1)
                nc.scalar.copy(tail_fT[:, f, :], tail_t(f)).then_inc(s_tail_c, 1)
            for n in range(2 * HC):
                act.wait_ge(s_tail, n + 3)
                nc.scalar.activation(tail_r[:, n, :], tail_h(n // HC, n % HC), ACT.Relu).then_inc(s_tail_r, 1)

        @block.tensor
        def _(pe):
            pe.wait_ge(s_const, 2)
            pe.wait_ge(s_lw, 64)
            nc.tensor.transpose(o_ps[0:RANK, 0:RANK], fb_sb[:, :], ident[0:RANK, 0:RANK])
            for c in range(HC):
                last = nc.tensor.transpose(o_ps[0:RANK, HALF + P * c:HALF + P * (c + 1)], u_sb[:, c, :], ident[:, :])
            last.then_inc(s_lt, 1)
            pe.wait_ge(s_lr, 1)
            nc.tensor.matmul(aux_ps[0:RANK, 0:C], fbT[:, :], v_sb[:, :], start=True, stop=True).then_inc(s_lt, 1)
            pe.wait_ge(s_lr, 2)
            nc.tensor.matmul(o_ps[:, 0:HID], fbv[:, :], uT[:, :], start=True, stop=True).then_inc(s_lt, 1)
            pe.wait_ge(s_norm, 1)
            for t in range(TILES):
                last = nc.tensor.transpose(score_ps[0][:, P * t:P * (t + 1)], XN[:, t, :], ident[:, :])
            last.then_inc(s_xt, 1)
            pe.wait_ge(s_bt, 1)
            nc.tensor.transpose(aux_ps[0:BOUNDS, 0:P], bounds[:, :], ident[:, :]).then_inc(s_btt, 1)
            pe.wait_ge(s_flag, 1)
            general = pe.value_load(flag[0:1, 0:1], min_val=0, max_val=1)

            def score(k, jt, h, ps, left, right, rows):
                r = h % 2
                for half in range(2):
                    last = nc.tensor.matmul(
                        ps[:, HALF * half:HALF * (half + 1)],
                        left[k][64 * r:64 * r + rows, h // 2, P * jt:P * (jt + 1)],
                        right[k][64 * r:64 * r + rows, h // 2, HALF * half:HALF * (half + 1)],
                        start=True, stop=True, tile_position=(64 * r, 0))
                return last

            with pe.If(general == 1):
                with pe.Fori(0, LATER) as i:
                    pe.wait_ge(general_later[2], i + 1)
                    transpose_later(pe, i, general_later)
                with pe.Fori(0, GROUPS) as g:
                    pe.wait_ge(m_load, PARTS_LOADED * (g + 1))
                    for n in range(HG * TILES):
                        h, it = n // TILES, n % TILES
                        pe.wait_ge(m_max, 32 * g + n + 1)
                        score(0, it, h, score_ps[n % 2], QT, KT, ROWS).then_inc(m_S, 1)
                    pe.wait_ge(m_max, 32 * g + 34)
                    nc.tensor.transpose(aux_ps[0:HG * TILES, 0:P], rmax[:, :, :].rearrange("p h t -> p (h t)"),
                                        ident[:, :]).then_inc(m_t, 1)
                pe.wait_ge(m_load, PARTS_LOADED * (GROUPS + 1))

            def unit(k, n):
                score(k, n // HG, n % HG, score_ps[n % 2], KT, QT, SROWS).then_inc(s_S, 1)

            def pv(k, jt, half):
                for h in range(HG):
                    last = nc.tensor.matmul(
                        o_ps[VW * h:VW * (h + 1), HALF * half:HALF * (half + 1)], V[k][:, jt, h, :],
                        E[:, jt % 2, h, HALF * half:HALF * (half + 1)],
                        start=(jt == 0), stop=(jt == TILES - 1), tile_position=(0, VW * h))
                last.then_inc(s_pv, 1)

            def ffn_transpose(chunk):
                pe.wait_ge(s_fn, chunk + 1)
                for t in range(FT):
                    last = nc.tensor.transpose(aux_ps[:, P * t:P * (t + 1)], fn[:, t, :], ident[:, :])
                last.then_inc(s_fT, 1)

            def ffn_hidden(chunk, c):
                if c == 0:
                    pe.wait_ge(s_fTc, chunk + 1)
                last = nc.tensor.matmul(aux_ps[:, FT * P * c:FT * P * (c + 1)], W1[:, P * c:P * (c + 1)],
                                        fT[:, :], start=True, stop=True)
                if c == HC - 1:
                    last.then_inc(s_fc, 1)

            def ffn_project(chunk, t):
                if t == 0:
                    pe.wait_ge(s_relu2, chunk + 1)
                for c in range(HC):
                    last = nc.tensor.matmul(aux_ps[:, P * t:P * (t + 1)], relu2[:, c, P * t:P * (t + 1)],
                                            W2[:, c, :], start=(c == 0), stop=(c == HC - 1))
                if t == FT - 1:
                    last.then_inc(s_fp, 1)

            def group(s, k, ffn, last_group=False):
                g = 2 * s + k
                chunk = g - LAG
                for jt in range(TILES):
                    if jt == 0:
                        pe.wait_ge(s_v[k], s + (1 if k == 0 else 3))
                        pe.wait_ge(s_ev, 2 * g + 2)
                    for half in range(2):
                        n = HG * (jt + 1) + 2 * half
                        pv(k, jt, half)
                        for m in (n + 2, n + 3):
                            if m < 32:
                                pe.wait_ge(s_E, 32 * g + m - 1)
                                unit(k, m)
                            elif not last_group:
                                if m == 32:
                                    pe.wait_ge(s_qk[1 - k], LOADED * (s + 1 + k))
                                pe.wait_ge(s_E, 32 * g + m - 1)
                                unit(1 - k, m - 32)
                            elif half == 1 or m > 32:
                                pe.wait_ge(s_E, 32 * g + 32)
                        if ffn:
                            if (jt, half) == (1, 0):
                                pe.wait_ge(s_att, g + 1)
                                ffn_transpose(chunk)
                            if jt in (2, 3):
                                ffn_hidden(chunk, 2 * (jt - 2) + half)
                            if jt == 5:
                                ffn_project(chunk, half)
                        elif (jt, half) == (1, 0):
                            pe.wait_ge(s_att, g + 1)
                            transpose_later(pe, g, main_later)
                        elif (k, jt, half) == (1, 6, 0):
                            pe.wait_ge(main_later[2], g + 2)
                            pe.wait_ge(s_ws, s + 1)
                            for c in range(HC):
                                last = nc.tensor.transpose(aux_ps[:, P * c:P * (c + 1)], staged_w[:, P * c:P * (c + 1)], ident[:, :])
                            last.then_inc(s_wt, 1)
                if ffn:
                    pe.wait_ge(s_y, chunk + 1)
                elif k == 0:
                    pe.wait_ge(main_later[2], g + 2)
                else:
                    pe.wait_ge(s_wd, s + 2)
                for t in range(TILES):
                    if t % 4 == 0:
                        pe.wait_ge(s_ev, 2 * g + 3 + t // 4)
                    last = nc.tensor.transpose(aux_ps[:, P * t:P * (t + 1)], o_sb[:, P * t:P * (t + 1)], ident[:, :])
                last.then_inc(s_to, 1)

            for n in range(WARM_UP):
                nc.tensor.matmul(o_ps[:, 0:HALF], split[:, 3, 0:P], split[:, 3, 0:HALF], start=True, stop=True)
            pe.wait_ge(s_qk[0], LOADED)
            for n in range(6):
                if n >= 2:
                    for _ in range(2):
                        nc.tensor.matmul(o_ps[:, 0:HALF], split[:, 3, 0:P], split[:, 3, 0:HALF], start=True, stop=True)
                    pe.wait_ge(s_E, n - 1)
                unit(0, n)
            with pe.Fori(0, 2) as s:
                for k in range(2):
                    group(s, k, False)
            with pe.Fori(2, STEPS - 1) as s:
                for k in range(2):
                    group(s, k, True)
            group(STEPS - 1, 0, True)
            group(STEPS - 1, 1, True, last_group=True)
            for f in range(2):
                pe.wait_ge(s_tail_n, f + 1)
                for t in range(TAIL):
                    last = nc.tensor.transpose(tail_t(f)[:, P * t:P * (t + 1)], tail_fn[:, TAIL * f + t, :], ident[:, :])
                last.then_inc(s_tail, 1)
            for f in range(2):
                pe.wait_ge(s_tail_c, 2)
                for c in range(HC):
                    nc.tensor.matmul(tail_h(f, c), W1[:, P * c:P * (c + 1)], tail_fT[:, f, :],
                                     start=True, stop=True).then_inc(s_tail, 1)
            for f in range(2):
                pe.wait_ge(s_tail_r2[0], 2 * f + 2)
                pe.wait_ge(s_tail_r2[1], 2 * f + 2)
                for t in range(TAIL):
                    for c in range(HC):
                        last = nc.tensor.matmul(tail_h(f, 0)[:, P * t:P * (t + 1)], tail_r2[:, HC * f + c, P * t:P * (t + 1)],
                                                W2[:, c, :], start=(c == 0), stop=(c == HC - 1))
                last.then_inc(s_tail, 1)

        class Chain:

            def __init__(self, dve, done, before=0):
                self.dve, self.done, self.before, self.n = dve, done, before, 0

            def then(self, ins):
                ins.then_inc(self.done, 1)
                self.n += 1

            def ready(self):
                self.dve.wait_ge(self.done, self.before + self.n)

            def link(self, ins):
                self.then(ins)
                self.ready()

        def layernorm_rstd(dve, ch, mvs, v, r, t):
            ch.link(nc.vector.tensor_scalar(v, mvs[:, :, 1:2].rearrange("p t o -> p (t o)"), EPS, None, ALU.add))
            ch.link(nc.vector.tensor_scalar(t.bitcast(I32), v.bitcast(I32), 1, None, ALU.logical_shift_right))
            ch.link(nc.vector.tensor_scalar(r.bitcast(I32), t.bitcast(I32), -1.0, MAGIC, ALU.mult, ALU.add))
            for _ in range(3):
                ch.link(nc.vector.scalar_tensor_tensor(out=t, in0=r, scalar=-0.5, in1=r, op0=ALU.mult, op1=ALU.mult))
                ch.link(nc.vector.tensor_tensor(out=t, in0=t, in1=v, op=ALU.mult))
                ch.link(nc.vector.scalar_tensor_tensor(out=r, in0=t, scalar=1.5, in1=r, op0=ALU.add, op1=ALU.mult))

        RSQRT_LINKS = 12

        @block.vector
        def _(dve):
            ch = Chain(dve, c_pre)
            for i, (done, n) in enumerate(((m_max, 2), (m_store, 64), (s_ev, 2), (s_att, 1), (s_out[0], 16), (s_out[1], 16),
                                           (main_later[1], 1), (main_later[2], 1), (main_later[4], 16),
                                           (general_later[1], 1), (general_later[2], 1), (general_later[4], 16))):
                nc.vector.memset(credit[:, i:i + 1], 0.0).then_inc(done, n)

            def statistics(b):
                dve.wait_ge(s_x[b], 16)
                for t in range(TILES * b, TILES * (b + 1)):
                    ch.then(nc.vector.bn_stats(bn[:, t, :], X[:, t, :]))
                ch.ready()
                for t in range(TILES * b, TILES * (b + 1)):
                    ch.then(nc.vector.bn_aggr(mv[:, t, :], bn[:, t, :]))

            def rstds(b0, b1):
                ch.ready()
                tiles = slice(TILES * b0, TILES * b1)
                layernorm_rstd(dve, ch, mv[:, tiles, :], var[:, tiles], rstd[:, tiles], nt[:, tiles])

            def norm(b):
                for t in range(TILES * b, TILES * (b + 1)):
                    last = nc.vector.tensor_scalar(XN[:, t, :], X[:, t, :], mv[:, t, 0:1], rstd[:, t:t + 1],
                                                   ALU.subtract, ALU.mult)
                last.then_inc(s_norm, 1)

            def bound(b):
                dve.wait_ge(s_wsq, b + 1)
                ch.link(nc.vector.tensor_reduce(by_tile[:, :, :], weighted(b).rearrange("p t (h d) -> p t h d", d=D), AX_X, ALU.add))
                ch.link(nc.vector.tensor_reduce(bounds[:, 1 + H * b:1 + H * (b + 1)],
                                                by_tile[:, :, :].rearrange("p t h -> p h t"), AX_X, ALU.max))

            statistics(0)
            rstds(0, 1)
            norm(0)
            dve.wait_ge(s_wc, 64)
            ch.then(nc.vector.scalar_tensor_tensor(out=w_c[:, :], in0=rot_c[:, :], scalar=float(D) ** -0.5,
                                                   in1=ent_c[:, :], op0=ALU.mult, op1=ALU.mult))
            ch.link(nc.vector.scalar_tensor_tensor(out=w_r[:, :], in0=rot_r[:, :], scalar=float(D) ** -0.5,
                                                   in1=ent_r[:, :], op0=ALU.mult, op1=ALU.mult))
            nc.vector.scalar_tensor_tensor(out=wabs[:, :], in0=w_r[:, :], scalar=-1.0, in1=w_r[:, :],
                                           op0=ALU.mult, op1=ALU.max).then_inc(s_wabs, 1)
            statistics(1)
            dve.wait_ge(s_split, 2)
            nc.vector.tensor_tensor(out=rest_k[:, :], in0=score_ps[0], in1=split[:, 3, :], op=ALU.subtract).then_inc(s_rest_k, 1)
            statistics(2)
            dve.wait_ge(s_split, 4)
            nc.vector.tensor_tensor(out=split[:, 5, :], in0=rest_k[:, :], in1=split[:, 4, :], op=ALU.subtract).then_inc(s_klow, 1)
            statistics(3)
            rstds(1, B)
            nc.vector.scalar_tensor_tensor(out=nmr[:, TILES:], in0=mv[:, TILES:, 0:1].rearrange("p t o -> p (t o)"),
                                           scalar=-1.0, in1=rstd[:, TILES:], op0=ALU.mult, op1=ALU.mult).then_inc(s_stat, 1)
            for b in range(B):
                bound(b)
            nc.vector.tensor_reduce(bounds[:, 0:1], bounds[:, 1:BOUNDS], AX_X, ALU.max).then_inc(s_bt, 1)
            dve.wait_ge(s_btt, 1)
            ch.link(nc.vector.tensor_reduce(bmax[:, :], aux_ps[0:BOUNDS, 0:P], AX_X, ALU.max))
            nc.vector.tensor_scalar(flag[:, :], bmax[0:1, :], SHIFT_LIMIT, None, ALU.is_gt).then_inc(s_flag, 1)
            ch.link(nc.vector.tensor_scalar(bneg[:, :], bmax[:, :], -1.01, -1e-3, ALU.mult, ALU.add))
            dve.wait_ge(s_preset, 2)
            nc.vector.tensor_scalar(shift_rows[:, 0, :], zrow[:, :], bneg[:, 0:1], None, ALU.add).then_inc(s_shr, 1)
            dve.wait_ge(s_flag, 1)
            general = dve.value_load(flag[0:1, 0:1], min_val=0, max_val=1)
            for b in range(1, B):
                norm(b)
            with dve.If(general == 1):
                with dve.Fori(0, LATER) as i:
                    chain = Chain(dve, c_split, SPLIT_LINKS * i)
                    split_later(dve, chain, i, general_later)
                    assert chain.n == SPLIT_LINKS
                with dve.Fori(0, GROUPS) as g:
                    for n in range(HG * TILES):
                        dve.wait_ge(m_S, 32 * g + n + 1)
                        nc.vector.tensor_reduce(rmax[:, n // TILES, n % TILES:n % TILES + 1], score_ps[n % 2],
                                                AX_X, ALU.max).then_inc(m_max, 1)
                    gc = Chain(dve, c_general, 5 * g)
                    dve.wait_ge(m_t, g + 1)
                    gc.link(nc.vector.tensor_scalar(nmax[:, :], aux_ps[0:HG * TILES, 0:P], -1.0, None, ALU.mult))
                    gc.link(nc.vector.tensor_copy(nparts[:, 0, :], nmax[:, :]))
                    gc.link(nc.vector.tensor_tensor(out=nres[:, :], in0=nmax[:, :], in1=nparts[:, 0, :], op=ALU.subtract))
                    gc.link(nc.vector.tensor_copy(nparts[:, 1, :], nres[:, :]))
                    gc.link(nc.vector.tensor_tensor(out=nmax[:, :], in0=nres[:, :], in1=nparts[:, 1, :], op=ALU.subtract))
                    nc.vector.tensor_copy(nparts[:, 2, :], nmax[:, :]).then_inc(m_parts, 1)

            wc = Chain(dve, c_weights)
            dve.wait_ge(s_w, 32)

            def ternary(w, rows, width):
                a = wa[:, :].rearrange("p (t c) -> p t c", t=rows)
                m = wb[:, :].rearrange("p (t c) -> p t c", t=rows)

                def wide(x):
                    return x[:, 0:rows].rearrange("p (t o) -> p t o", o=1).to_broadcast([P, rows, width])

                wc.link(nc.vector.tensor_reduce(ws[:, 0:rows], w, AX_X, ALU.add, apply_absolute_value=True))
                wc.link(nc.vector.tensor_scalar(ws[:, 0:rows], ws[:, 0:rows], 1.0 / width, EPS, ALU.mult, ALU.max))
                wc.then(nc.vector.tensor_scalar(wh[:, 0:rows], ws[:, 0:rows], 0.5, None, ALU.mult))
                wc.link(nc.vector.tensor_scalar(wnh[:, 0:rows], ws[:, 0:rows], -0.5, None, ALU.mult))
                wc.then(nc.vector.tensor_tensor(out=a, in0=w, in1=wide(wh), op=ALU.is_gt))
                wc.link(nc.vector.tensor_tensor(out=m, in0=w, in1=wide(wnh), op=ALU.is_lt))
                wc.link(nc.vector.tensor_tensor(out=a, in0=a, in1=m, op=ALU.subtract))
                wc.link(nc.vector.tensor_tensor(out=m, in0=a, in1=w, op=ALU.subtract))
                wc.link(nc.vector.tensor_tensor(out=a, in0=m, in1=w, op=ALU.add))
                wc.link(nc.vector.tensor_tensor(out=w, in0=a, in1=wide(ws), op=ALU.mult))

            ternary(wfc, HC, C)
            ternary(wpj.rearrange("p (t c) -> p t c", t=1), 1, HID)
            nc.vector.memset(wh[:, :], 0.0).then_inc(s_wd, 1)

            def finish_group(chain, s, k):
                g = 2 * s + k
                for half in range(2):
                    dve.wait_ge(s_pv, 16 * g + 15 + half)
                    nc.vector.tensor_copy(o_sb[:, HALF * half:HALF * (half + 1)],
                                          o_ps[:, HALF * half:HALF * (half + 1)]).then_inc(s_ev, 1)
                dve.wait_ge(s_to, g + 1)
                heads = aux_ps.rearrange("p (t h v) -> p t h v", t=TILES, h=HG)
                chain.link(nc.vector.reciprocal(rden[:, :, :], heads[:, :, :, D:D + 1].rearrange("p t h o -> p t (h o)")))
                nc.vector.tensor_tensor(
                    out=att[:, :, :, :].rearrange("p t h d -> p (t h) d"),
                    in0=aux_ps.rearrange("p (th v) -> p th v", v=VW)[:, :, 0:D],
                    in1=rden[:, :, :].rearrange("p t (h o) -> p (t h) o", o=1).to_broadcast([P, TILES * HG, D]),
                    op=ALU.mult).then_inc(s_att, 1)
                dve.wait_ge(s_att, g + 2)
                xs = X[:, bass.ds(TILES * (s // 2), TILES), bass.ds(64 * (s % 2) + 32 * k, HG * D)]
                chain.link(nc.vector.tensor_tensor(out=xs, in0=xs, in1=att[:, :, :, :].rearrange("p t h d -> p t (h d)"),
                                                   op=ALU.add))

            FINISH_LINKS = 2

            def ffn(chain, pair, k):
                chunk = 2 * pair + k

                def tile(t):
                    return X[:, bass.ds(FT * chunk + t, 1), :].rearrange("p t c -> p (t c)")

                for t in range(FT):
                    chain.then(nc.vector.bn_stats(fbn[:, t, :], tile(t)))
                chain.ready()
                chain.then(nc.vector.memset(fnt[:, :], 0.0))
                for t in range(FT):
                    chain.then(nc.vector.bn_aggr(fmv[:, t, :], fbn[:, t, :]))
                chain.ready()
                layernorm_rstd(dve, chain, fmv, fvar[:, :], frstd[:, :], fnt[:, :])
                for t in range(FT):
                    last = nc.vector.tensor_scalar(fn[:, t, :], tile(t), fmv[:, t, 0:1], frstd[:, t:t + 1],
                                                   ALU.subtract, ALU.mult)
                last.then_inc(s_fn, 1)
                dve.wait_ge(s_fT, chunk + 1)
                nc.vector.tensor_copy(fT[:, :], aux_ps[:, 0:FT * P]).then_inc(s_fTc, 1)
                dve.wait_ge(s_fc, chunk + 1)
                nc.vector.tensor_scalar(relu[:, :, :].rearrange("p c n -> p (c n)"), aux_ps, 0.0, None,
                                        ALU.max).then_inc(s_relu, 1)
                dve.wait_ge(s_fp, chunk + 1)
                dve.wait_ge(s_out[k], 16 * pair + 16)
                nc.vector.tensor_tensor(
                    out=y[k][:, :, :], in0=aux_ps[:, 0:FT * P].rearrange("p (t c) -> p t c", c=C),
                    in1=X[:, bass.ds(FT * chunk, FT), :], op=ALU.add).then_inc(s_y, 1)

            FFN_LINKS = 2 * FT + RSQRT_LINKS + 1

            each = SPLIT_LINKS + FINISH_LINKS
            with dve.Fori(0, LATER // 2) as s:
                for k in range(2):
                    chain = Chain(dve, c_first, each * (2 * s + k))
                    split_later(dve, chain, 2 * s + k, main_later)
                    if k == 1:
                        dve.wait_ge(s_wt, s + 1)
                        nc.vector.tensor_copy(weights_T[:, bass.ds(s, 1), :].rearrange("p o n -> p (o n)"),
                                              aux_ps[:, 0:HID]).then_inc(s_wd, 1)
                    finish_group(chain, s, k)
            dve.wait_ge(s_wd, 3)
            dve.wait_ge(s_lr, 3)
            nc.vector.tensor_tensor(out=W1, in0=W1, in1=low_rank[:, :], op=ALU.add)
            each = FINISH_LINKS + FFN_LINKS
            with dve.Fori(2, STEPS - 1) as s:
                for k in range(2):
                    chain = Chain(dve, c_mid, each * (2 * s + k - LAG))
                    ffn(chain, s - LAG // 2, k)
                    finish_group(chain, s, k)
                    assert chain.n == each
            chain = Chain(dve, c_last)
            for k in range(2):
                ffn(chain, STEPS - 1 - LAG // 2, k)
                finish_group(chain, STEPS - 1, k)
            first, tc = (B - 1) * TILES, Chain(dve, c_tail)
            for t in range(TILES):
                tc.then(nc.vector.bn_stats(bn[:, t, :], X[:, first + t, :]))
            tc.ready()
            tc.then(nc.vector.memset(nt[:, 0:TILES], 0.0))
            for t in range(TILES):
                tc.then(nc.vector.bn_aggr(mv[:, t, :], bn[:, t, :]))
            tc.ready()
            layernorm_rstd(dve, tc, mv[:, 0:TILES, :], var[:, 0:TILES], rstd[:, 0:TILES], nt[:, 0:TILES])
            for t in range(TILES):
                last = nc.vector.tensor_scalar(tail_fn[:, t, :], X[:, first + t, :], mv[:, t, 0:1], rstd[:, t:t + 1],
                                               ALU.subtract, ALU.mult)
                if t % TAIL == TAIL - 1:
                    last.then_inc(s_tail_n, 1)
            for n in range(0, 2 * HC, 2):
                square_tail(dve, nc.vector, n)
            for f in range(2):
                dve.wait_ge(s_tail, 3 + 2 * HC + f)
                nc.vector.tensor_tensor(
                    out=tail_y[:, TAIL * f:TAIL * (f + 1), :], in0=tail_h(f, 0).rearrange("p (t c) -> p t c", c=C),
                    in1=X[:, first + TAIL * f:first + TAIL * (f + 1), :], op=ALU.add).then_inc(s_tail_y, 1)


_INS = ["L0_attn_inputs", "L0_attn_rotation_params", "L0_attn_entangle_params", "L0_ffn_fast_b",
        "L0_ffn_w_fc", "L0_ffn_w_proj", "L0_ffn_u", "L0_ffn_v", "L0_ffn_gate"]


def kernel(**inputs):
    import numpy as _np
    import concourse.bacc as _bacc
    from concourse import mybir as _mybir
    from concourse.bass_utils import run_bass_kernel_spmd as _run

    nc = _bacc.Bacc("TRN2", target_bir_lowering=False, num_devices=1)
    arrays, args = {}, []
    for name in _INS:
        a = _np.ascontiguousarray(inputs[name])
        a = a.reshape(1) if a.ndim == 0 else a
        arrays[f"in_{name}_dram"] = a
        args.append(nc.dram_tensor(f"in_{name}_dram", a.shape, _mybir.dt.from_np(a.dtype), kind="ExternalInput").ap())
    args.append(nc.dram_tensor("out_0_dram", (B, T, C), _mybir.dt.float32, kind="ExternalOutput").ap())
    build(nc, *args)
    r = _run(nc, [arrays], core_ids=[0])
    return r.results[0]["out_0_dram"]
```

```python
from contextlib import ExitStack

import concourse.bass as bass
from concourse import mybir

F32, BF16, I32 = mybir.dt.float32, mybir.dt.bfloat16, mybir.dt.int32
ACT = mybir.ActivationFunctionType
ALU = mybir.AluOpType
AX_X = mybir.AxisListType.X

B, T, C, H = 4, 1024, 128, 16
D = C // H
P = 128
TILES = T // P
HG = 4
GROUPS = B * H // HG
STEPS = GROUPS // 2
HALF = 512
HT = TILES // 2
SWEEPS = 2
UNITS = 2 * TILES * SWEEPS
BANKS = 3
SLOTS = 4
AHEAD = 5
PARTS = 6
ROWS = 6 * D
SROWS = ROWS + 3
VW = 32
HID, RANK = 512, 16
HC = HID // P
FT = 2
EPS = 1e-5
SHIFT_LIMIT = 40.0
MAGIC = float(0x5F3759DF)
WARM_UP = [12, 12]
SPLIT_TILES = 3
ST = SPLIT_TILES * P
BOUNDS = 1 + B * H
TAIL = TILES // 2
FFN_AT = [3, 4, 5, 6, 6, 12, 13]
LAG = 4


def build(nc, x_in, rot, ent, fast_b, w_fc, w_proj, u_in, v_in, gate, out):
    q_dram = nc.dram_tensor("q_scratch", (C, 6, B * T), BF16, kind="Internal").ap()
    k_dram = nc.dram_tensor("k_scratch", (C, 6, B * T), BF16, kind="Internal").ap()
    shift_dram = nc.dram_tensor("shift_scratch", (B * H, 3, T), BF16, kind="Internal").ap()

    with ExitStack() as ctx:
        def sb(name, shape, dt=F32):
            return ctx.enter_context(nc.sbuf_tensor(name, shape, dt))

        def sem(name):
            return ctx.enter_context(nc.semaphore(name))

        psum = ctx.enter_context(nc.psum_tensor("psum", [P, 4096], F32))
        score_ps = [psum[:, 1024 * i:1024 * (i + 1)] for i in range(BANKS)]
        o_ps = psum[:, 3072:3584]
        aux_ps = psum[:, 3584:4096]

        X = sb("X", [P, B * TILES, C])
        XN = sb("XN", [P, B * TILES, C])
        staged = sb("staged", [P, SPLIT_TILES, C])
        split = sb("split", [P, PARTS, T], BF16)
        wx, rest_k, rest_q = (sb(n, [P, T]) for n in ("wx", "rest_k", "rest_q"))
        later = sb("later_split", [P, PARTS, ST], BF16)
        later_wx, later_k, later_q = (sb(n, [P, ST]) for n in ("later_wx", "later_rest_k", "later_rest_q"))
        bounds = sb("bounds", [P, BOUNDS])
        by_tile = sb("bounds_by_tile", [P, TILES, H])
        shift_row = sb("shift_row", [BOUNDS, T], BF16)
        QT = [sb(f"QT{k}", [P, 2, T], BF16) for k in range(2)]
        KT = [sb(f"KT{k}", [P, 2, T], BF16) for k in range(2)]
        V = [sb(f"V{k}", [P, TILES, HG, VW]) for k in range(2)]
        E = sb("E", [P, SLOTS, HG, HALF])
        o_sb = sb("o_sb", [P, HALF])
        att = sb("att", [P, HT, HG, D])
        rden = sb("rden", [P, HT, HG])
        bn = sb("bn", [P, B * TILES, 6])
        mv = sb("mv", [P, B * TILES, 2])
        var = sb("var", [P, B * TILES])
        rstd = sb("rstd", [P, B * TILES])
        nt = sb("nt", [P, B * TILES])
        nmr = sb("neg_mean_over_deviation", [P, B * TILES])
        fbn, fmv = sb("fbn", [P, FT, 6]), sb("fmv", [P, FT, 2])
        fvar, frstd, fnt = sb("fvar", [P, FT]), sb("frstd", [P, FT]), sb("fnt", [P, FT])
        fn = sb("fn", [P, FT, C])
        fT = sb("fT", [P, FT * P])
        relu = sb("relu", [P, HC, FT * P])
        relu2 = sb("relu2", [P, HC, FT * P])
        y = [sb(f"y{k}", [P, FT, C]) for k in range(2)]
        ident = sb("ident", [P, P])
        rot_c, ent_c, w_c = (sb(n, [P, 1]) for n in ("rot_c", "ent_c", "w_c"))
        rot_r, ent_r, w_r, wabs = (sb(n, [P, C]) for n in ("rot_r", "ent_r", "w_r", "w_abs"))
        credit = sb("credit", [P, 16])
        bmax = sb("bmax", [BOUNDS, 1])
        bneg = sb("bneg", [BOUNDS, 1])
        flag = sb("flag", [1, 1], I32)
        zrow = sb("zrow", [BOUNDS, T], BF16)
        weights = sb("weights", [P, 2, HID])
        wfc = weights[:, 0, :].rearrange("p (c n) -> p c n", c=HC)
        wpj = weights[:, 1, :]
        staged_w = sb("staged_weights", [P, HID])
        weights_T = sb("weights_T", [P, 2, HID])
        W1 = weights_T[:, 0, :]
        W2 = weights_T[:, 1, :].rearrange("p (c n) -> p c n", c=HC)
        wa, wb = sb("wa", [P, 512]), sb("wb", [P, 512])
        ws, wh = sb("ws", [P, HC]), sb("wh", [P, HC])
        wnh = sb("wnh", [P, HC])
        u_sb = sb("u_sb", [P, HC, RANK])
        v_sb = sb("v_sb", [RANK, C])
        fb_sb = sb("fb_sb", [RANK, RANK])
        fbT = sb("fbT", [RANK, RANK])
        fbv = sb("fbv", [RANK, C])
        uT = sb("uT", [RANK, HID])
        gate_c = sb("gate_c", [RANK, 1])
        low_rank = sb("low_rank", [P, HID])
        rmax = sb("rmax", [P, HG, TILES])
        nmax = sb("nmax", [HG * TILES, P])
        nres = sb("nres", [HG * TILES, P])
        nparts = sb("nparts", [HG * TILES, 3, P], BF16)

        s_x = [sem(f"s_x{b}") for b in range(B)]
        s_w = sem("s_weights_loaded")
        s_lw = sem("s_low_rank_weights_loaded")
        s_wc = sem("s_rot_ent_loaded")
        s_const = sem("s_constants")
        s_preset = sem("s_operands_preset")
        s_norm = sem("s_normed")
        s_xt = sem("s_x_transposed")
        s_split = sem("s_act_split")
        s_rest_k = sem("s_rest_k")
        s_rest_q = sem("s_rest_q")
        s_klow = sem("s_k_low_part")
        s_qlow = sem("s_q_low_part")
        s_parts = sem("s_parts_stored")
        s_stat = sem("s_statistics")
        s_sq = [sem(f"s_squares{b}") for b in range(B)]
        s_wsq = [sem(f"s_weighted_squares{b}") for b in range(B)]
        s_bt = sem("s_bounds_by_token")
        s_btt = sem("s_bounds_transposed")
        s_shr = sem("s_shift_rows")
        s_first = [sem(f"s_first_shifts{k}") for k in range(2)]
        s_shift = sem("s_shift_stored")
        s_flag = sem("s_flag")
        s_lt = sem("s_low_rank_product")
        s_lr = sem("s_low_rank_copied")
        later_sems = [[sem(f"{m}_later_{n}") for n in ("staged", "transposed", "read", "split", "stored")]
                      for m in "sm"]
        s_qk = [sem(f"s_qk{k}") for k in range(2)]
        s_v = [sem(f"s_v{k}") for k in range(2)]
        s_S = sem("s_scores")
        s_E = sem("s_exps")
        s_pv = sem("s_pv")
        s_ev = sem("s_o_evacuated")
        s_to = sem("s_o_transposed")
        s_att = sem("s_attention_read")
        s_tail_t = sem("s_tail_transposed")
        s_tail_h = sem("s_tail_hidden")
        s_tail_p = sem("s_tail_projected")
        s_tail_n = sem("s_tail_normed")
        s_tail_c = sem("s_tail_copied")
        s_tail_r = sem("s_tail_relu")
        s_tail_r2_act, s_tail_r2_pool, s_tail_r2_dve = (sem(f"s_tail_relu2_{n}") for n in ("scalar", "gpsimd", "vector"))
        s_tail_out = [sem(f"s_tail_out_stored{f}") for f in range(2)]
        s_wabs = sem("s_w_abs")
        s_tail_y = sem("s_tail_y")
        s_fTc = sem("s_ffn_transposed_copied")
        s_fn = sem("s_ffn_normed")
        s_fT = sem("s_ffn_transposed")
        s_fc = sem("s_ffn_hidden")
        s_relu = sem("s_ffn_relu")
        s_relu2 = sem("s_ffn_relu2")
        s_fp = sem("s_ffn_projected")
        s_y = sem("s_y")
        s_out = [sem(f"s_out_stored{k}") for k in range(2)]
        s_ws = sem("s_weights_staged")
        s_wt = sem("s_weights_transposed")
        s_wd = sem("s_weights_copied")
        c_pre, c_split, c_general, c_first, c_mid, c_weights, c_last, c_tail = (
            sem(f"c_{n}") for n in ("pre", "split", "general", "first", "mid", "weights", "last", "tail"))
        m_load = sem("m_operands_loaded")
        m_S = sem("m_scores")
        m_max = sem("m_max")
        m_t = sem("m_max_transposed")
        m_parts = sem("m_max_parts")
        m_store = sem("m_shift_stored")

        def load_parts(sp, group, k, done):
            for r in range(2):
                for dst, src in ((QT[k], q_dram), (KT[k], k_dram)):
                    heads = src.rearrange("(x r d) t n -> r x d t n", r=2, d=D)[r]
                    sp.dma_start(dst[64 * r:64 * r + ROWS, :, :],
                                 heads[bass.ds(2 * (group % 4), 2), :, :, bass.ds(T * (group // 4), T)]
                                 .rearrange("x d t n -> (d t) x n")).then_inc(done, 16)

        def load_shifts(sp, group, k, done):
            for r in range(2):
                rows = 64 * r + ROWS
                sp.dma_start(QT[k][rows:rows + 3, :, :],
                             shift_dram.rearrange("(x r) p n -> r p x n", r=2)[r, :, bass.ds(2 * group, 2), :]).then_inc(done, 16)

        PARTS_LOADED = 4 * 16
        LOADED = 6 * 16

        def out_rows(chunk):
            return out.rearrange("b t c -> (b t) c")[bass.ds(chunk * (FT * P), FT * P), :].rearrange("(t p) c -> p t c", p=P)

        def store_parts(sp, parts, tokens, done):
            q, x, n = parts[:, 0:3, :], parts[:, 3:6, :], parts.shape[2]
            sp.dma_start(k_dram[:, 0:3, tokens], x[:, 0:1, :].to_broadcast([P, 3, n])).then_inc(done, 16)
            sp.dma_start(k_dram[:, 3:5, tokens], x[:, 1:2, :].to_broadcast([P, 2, n])).then_inc(done, 16)
            sp.dma_start(k_dram[:, 5:6, tokens], x[:, 2:3, :]).then_inc(done, 16)
            sp.dma_start(q_dram[:, 0:3, tokens], q).then_inc(done, 16)
            sp.dma_start(q_dram[:, 3:5, tokens], q[:, 0:2, :]).then_inc(done, 16)
            sp.dma_start(q_dram[:, 5:6, tokens], q[:, 0:1, :]).then_inc(done, 16)

        def stage_later(pool, i, sems):
            is_staged, transposed = sems[0], sems[1]
            pool.wait_ge(transposed, i + 1)
            nc.gpsimd.tensor_copy(staged[:, :, :], XN[:, bass.ds(TILES + SPLIT_TILES * i, SPLIT_TILES), :]).then_inc(is_staged, 1)

        def transpose_later(pe, i, sems):
            is_staged, transposed = sems[0], sems[1]
            pe.wait_ge(is_staged, i + 1)
            for t in range(SPLIT_TILES):
                last = nc.tensor.transpose(aux_ps[:, P * t:P * (t + 1)], staged[:, t, :], ident[:, :])
            last.then_inc(transposed, 1)

        def split_later(dve, chain, i, sems):
            _, transposed, read, is_split, stored = sems
            x = aux_ps[:, 0:ST]
            dve.wait_ge(stored, 16 * PARTS * i + 16)
            dve.wait_ge(transposed, i + 2)
            chain.then(nc.vector.tensor_copy(later[:, 3, :], x))
            chain.link(nc.vector.tensor_scalar(later_wx[:, :], x, w_c[:, 0:1], None, ALU.mult))
            nc.vector.tensor_tensor(out=later_k[:, :], in0=x, in1=later[:, 3, :], op=ALU.subtract).then_inc(read, 1)
            chain.link(nc.vector.tensor_copy(later[:, 0, :], later_wx[:, :]))
            chain.then(nc.vector.tensor_tensor(out=later_q[:, :], in0=later_wx[:, :], in1=later[:, 0, :], op=ALU.subtract))
            dve.wait_ge(read, i + 2)
            chain.link(nc.vector.tensor_copy(later[:, 4, :], later_k[:, :]))
            chain.then(nc.vector.tensor_copy(later[:, 1, :], later_q[:, :]))
            chain.link(nc.vector.tensor_tensor(out=later[:, 5, :], in0=later_k[:, :], in1=later[:, 4, :], op=ALU.subtract))
            nc.vector.tensor_tensor(out=later[:, 2, :], in0=later_q[:, :], in1=later[:, 1, :],
                                    op=ALU.subtract).then_inc(is_split, 1)

        SPLIT_LINKS = 7

        def store_later(sp, i, sems):
            is_split, stored = sems[3], sems[4]
            sp.wait_ge(is_split, i + 1)
            store_parts(sp, later, bass.ds(T + ST * i, ST), stored)

        main_later, general_later = later_sems
        lr_ps = score_ps[1]
        LATER = (B - 1) * TILES // SPLIT_TILES
        assert LATER == SWEEPS * LAG

        block = ctx.enter_context(nc.Block())

        E_tiles = E[:, :, :, :].rearrange("p s h (t c) -> p (s h t) c", c=C)

        def squares(b):
            return E_tiles[:, TILES * b:TILES * (b + 1), :]

        def weighted(b):
            return E_tiles[:, TILES * (B + b):TILES * (B + b + 1), :]

        def norm(op, b, done):
            for t in range(TILES * b, TILES * (b + 1)):
                last = op(XN[:, t, :], X[:, t, :], mv[:, t, 0:1], rstd[:, t:t + 1], ALU.subtract, ALU.mult)
            last.then_inc(done, 1)

        def weight_squares(engine, op, b):
            engine.wait_ge(s_sq[b], 1)
            op(out=weighted(b), in0=squares(b), in1=wabs[:, :].rearrange("p (o c) -> p o c", o=1).to_broadcast([P, TILES, C]),
               op=ALU.mult).then_inc(s_wsq[b], 1)

        tail_r = E[:, 0:2, :, :].rearrange("p s h n -> p (s h) n")
        tail_r2 = E[:, 2:4, :, :].rearrange("p s h n -> p (s h) n")
        tail_fn = XN[:, 0:TILES, :]
        tail_y = XN[:, TILES:2 * TILES, :]
        tail_fT = rest_k[:, :].rearrange("p (f n) -> p f n", f=2)

        def tail_t(f):
            return score_ps[2][:, HALF * f:HALF * (f + 1)]

        def tail_h(f, c):
            return psum[:, 2048 * f + HALF * c:2048 * f + HALF * (c + 1)]

        def square_tail(engine, op, n, done):
            engine.wait_ge(s_tail_r, n + 1)
            op(out=tail_r2[:, n, :], in0=tail_r[:, n, :], in1=tail_r[:, n, :], op=ALU.mult).then_inc(done, 1)

        @block.sync
        def _(sp):
            for b in range(B):
                sp.dma_start(X[:, TILES * b:TILES * (b + 1), :],
                             x_in[b].rearrange("(t p) c -> p t c", p=P)).then_inc(s_x[b], 16)
                if b == 0:
                    sp.dma_start(rot_c[:, :], rot.rearrange("h (d o) -> (h d) o", o=1)).then_inc(s_wc, 16)
                    sp.dma_start(ent_c[:, :], ent.rearrange("h (d o) -> (h d) o", o=1)).then_inc(s_wc, 16)
                    for row, src in ((rot_r, rot), (ent_r, ent)):
                        sp.dma_start(row[:, :], src.rearrange("(a h) d -> a (h d)", a=1).to_broadcast([P, C])).then_inc(s_wc, 16)
                    sp.dma_start(u_sb[:, :, :], u_in.rearrange("(t p) r -> p t r", p=P)).then_inc(s_lw, 16)
                    sp.dma_start(v_sb[:, :], v_in).then_inc(s_lw, 16)
                    sp.dma_start(fb_sb[:, :], fast_b).then_inc(s_lw, 16)
                    sp.dma_start(gate_c[:, :], gate.rearrange("(a b) -> a b", a=1).to_broadcast([RANK, 1])).then_inc(s_lw, 16)
            sp.dma_start(wfc, w_fc.rearrange("(t p) c -> p t c", p=P)).then_inc(s_w, 16)
            sp.dma_start(wpj, w_proj).then_inc(s_w, 16)
            sp.wait_ge(s_preset, 2)
            for n in (1, 2):
                sp.dma_start(shift_dram[:, n, :], zrow[1:BOUNDS, :]).then_inc(s_shift, 16)
            sp.wait_ge(s_preset, 3)
            sp.wait_ge(s_split, 4)
            sp.wait_ge(s_klow, 1)
            sp.wait_ge(s_split, 5)
            sp.wait_ge(s_qlow, 1)
            store_parts(sp, split, slice(0, T), s_parts)
            sp.wait_ge(s_parts, 16 * PARTS)
            for k in range(2):
                load_parts(sp, k, k, s_qk[k])
            sp.wait_ge(s_shr, 1)
            for k in range(2):
                for h in range(HG):
                    row = 64 * (h % 2) + ROWS
                    sp.dma_start(QT[k][row:row + 1, h // 2, :], shift_row[1 + HG * k + h:2 + HG * k + h, :]).then_inc(s_first[k], 16)
            sp.dma_start(shift_dram[:, 0, :], shift_row[1:BOUNDS, :]).then_inc(s_shift, 16)
            sp.wait_ge(s_flag, 1)
            general = sp.value_load(flag[0:1, 0:1], min_val=0, max_val=1)
            with sp.If(general == 1):
                sp.wait_ge(s_shift, 48)
                with sp.Fori(0, LATER) as i:
                    store_later(sp, i, general_later)
                sp.wait_ge(general_later[4], 16 * PARTS * LATER + 16)
                with sp.Fori(0, GROUPS) as g:
                    sp.wait_ge(m_store, 16 * HG * g + 64)
                    load_parts(sp, g, 0, m_load)
                    sp.wait_ge(m_parts, g + 1)
                    for h in range(HG):
                        sp.dma_start(
                            shift_dram[bass.ds(HG * g + h, 1), :, :].rearrange("h p (t n) -> (h t) p n", n=P),
                            nparts[TILES * h:TILES * (h + 1), :, :]).then_inc(m_store, 16)
                sp.wait_ge(m_store, 16 * HG * GROUPS + 64)
                load_parts(sp, 0, 0, m_load)
                for k in range(2):
                    sp.wait_ge(s_first[k], 64)
                    load_shifts(sp, k, k, m_load)
            sp.wait_ge(s_shift, 48)

            def next_load(s, k):
                sp.wait_ge(s_S, 64 * s + 32 * k - 32)
                load_parts(sp, 2 * s + k, k, s_qk[k])
                load_shifts(sp, 2 * s + k, k, s_qk[k])

            def store(chunk, k):
                sp.wait_ge(s_y, chunk + 1)
                sp.dma_start(out_rows(chunk), y[k][:, :, :]).then_inc(s_out[k], 16)

            with sp.Fori(0, LAG // 2) as s:
                for k in range(2):
                    for half in range(SWEEPS):
                        store_later(sp, SWEEPS * (2 * s + k) + half, main_later)
                    sp.wait_ge(main_later[4], 16 * PARTS * SWEEPS * (2 * s + k) + 16 * PARTS * SWEEPS + 16)
                    next_load(s + 1, k)
            with sp.Fori(3, STEPS) as s:
                for k in range(2):
                    next_load(s, k)
                    store(2 * s + k - 6, k)
            for k in range(2):
                store(2 * STEPS + k - 6, k)
            for f in range(2):
                sp.wait_ge(s_tail_y, f + 1)
                first = (B - 1) * TILES + TAIL * f
                sp.dma_start(out.rearrange("b t c -> (b t) c")[P * first:P * (first + TAIL), :]
                             .rearrange("(t p) c -> p t c", p=P), tail_y[:, TAIL * f:TAIL * (f + 1), :]).then_inc(s_tail_out[f], 16)
            for k in range(2):
                sp.wait_ge(s_out[k], 16 + 16 * (GROUPS - LAG) // 2)
                sp.wait_ge(s_tail_out[k], 16)

        @block.gpsimd
        def _(pool):
            nc.gpsimd.memset(ident[:, :], 0.0).then_inc(s_const, 1)
            pool.wait_ge(s_const, 1)
            nc.gpsimd.affine_select(out=ident[:, :], in_=ident[:, :], compare_op=ALU.not_equal, fill=1.0,
                                    base=0, pattern=[[-1, P]], channel_multiplier=1).then_inc(s_const, 1)
            for k in range(2):
                last = nc.gpsimd.memset(KT[k][:, :, :], 1.0)
            last.then_inc(s_preset, 1)
            nc.gpsimd.memset(zrow[:, :], 0.0).then_inc(s_preset, 1)
            for k in range(2):
                last = nc.gpsimd.memset(QT[k][:, :, :], 0.0)
            last.then_inc(s_preset, 1)
            nc.gpsimd.memset(V[0][:, :, :, :], 0.0)
            nc.gpsimd.memset(V[1][:, :, :, :], 0.0).then_inc(s_v[1], 1)
            pool.wait_ge(s_v[1], 1)
            nc.gpsimd.memset(V[0][:, :, :, D:D + 1], 1.0)
            nc.gpsimd.memset(V[1][:, :, :, D:D + 1], 1.0).then_inc(s_v[1], 1)

            pool.wait_ge(s_split, 3)
            nc.gpsimd.tensor_tensor(out=rest_q[:, :], in0=wx[:, :], in1=split[:, 0, :],
                                    op=ALU.subtract).then_inc(s_rest_q, 1)
            pool.wait_ge(s_split, 5)
            nc.gpsimd.tensor_tensor(out=split[:, 2, :], in0=rest_q[:, :], in1=split[:, 1, :],
                                    op=ALU.subtract).then_inc(s_qlow, 1)
            pool.wait_ge(s_wabs, 1)
            for b in (0, 1):
                weight_squares(pool, nc.gpsimd.tensor_tensor, b)
            pool.wait_ge(s_flag, 1)
            general = pool.value_load(flag[0:1, 0:1], min_val=0, max_val=1)
            with pool.If(general == 1):
                pool.wait_ge(s_norm, B)
                with pool.Fori(0, LATER) as i:
                    stage_later(pool, i, general_later)
                pool.wait_ge(general_later[1], LATER + 1)

            def values(step, k):
                nc.gpsimd.tensor_copy(
                    V[k][:, :, :, 0:D],
                    XN[:, bass.ds(TILES * (step // 2), TILES), bass.ds(64 * (step % 2) + 32 * k, HG * D)]
                    .rearrange("p t (h d) -> p t h d", d=D)).then_inc(s_v[k], 1)

            def square(chunk):
                for part in range(2):
                    cs = slice(2 * part, 2 * part + 2)
                    pool.wait_ge(s_relu, 2 * chunk + 1 + part)
                    nc.gpsimd.tensor_tensor(out=relu2[:, cs, :], in0=relu[:, cs, :], in1=relu[:, cs, :],
                                            op=ALU.mult).then_inc(s_relu2, 1)

            pool.wait_ge(s_norm, B)
            values(0, 0)
            values(0, 1)
            with pool.Fori(0, LAG // 2) as s:
                for k in range(2):
                    stage_later(pool, SWEEPS * (2 * s + k), main_later)
                    if k == 1:
                        pool.wait_ge(s_wd, s + 1)
                        nc.gpsimd.tensor_copy(staged_w[:, :], weights[:, bass.ds(s, 1), :].rearrange("p o n -> p (o n)")).then_inc(s_ws, 1)
                    stage_later(pool, SWEEPS * (2 * s + k) + 1, main_later)
                    pool.wait_ge(s_pv, 32 * s + 16 * k + 16)
                    values(s + 1, k)
            with pool.Fori(2, STEPS - 1) as s:
                for k in range(2):
                    square(2 * s + k - LAG)
                    pool.wait_ge(s_pv, 32 * s + 16 * k + 16)
                    values(s + 1, k)
            for k in range(2):
                square(2 * STEPS - 2 + k - LAG)
            for n in range(0, 2 * HC, 2):
                square_tail(pool, nc.gpsimd.tensor_tensor, n, s_tail_r2_pool)

        @block.scalar
        def _(act):
            act.wait_ge(s_lt, 1)
            nc.scalar.copy(fbT[:, :], lr_ps[0:RANK, 0:RANK])
            nc.scalar.copy(uT[:, :], lr_ps[0:RANK, HALF:2 * HALF]).then_inc(s_lr, 1)
            act.wait_ge(s_lt, 2)
            act.wait_ge(s_lw, 64)
            nc.scalar.activation(fbv[:, :], aux_ps[0:RANK, 0:C], ACT.Copy, scale=gate_c[:, 0:1]).then_inc(s_lr, 1)
            act.wait_ge(s_lt, 3)
            nc.scalar.copy(low_rank[:, :], lr_ps[:, 0:HID]).then_inc(s_lr, 1)
            xT = score_ps[0]
            act.wait_ge(s_xt, 1)
            nc.scalar.copy(split[:, 3, :], xT).then_inc(s_split, 1)
            act.wait_ge(s_wabs, 1)
            nc.scalar.activation(wx[:, :], xT, ACT.Copy, scale=w_c[:, 0:1]).then_inc(s_split, 1)
            act.wait_ge(s_split, 2)
            nc.scalar.copy(split[:, 0, :], wx[:, :]).then_inc(s_split, 1)
            act.wait_ge(s_rest_k, 1)
            nc.scalar.copy(split[:, 4, :], rest_k[:, :]).then_inc(s_split, 1)
            act.wait_ge(s_rest_q, 1)
            nc.scalar.copy(split[:, 1, :], rest_q[:, :]).then_inc(s_split, 1)
            nc.scalar.activation(squares(0), XN[:, 0:TILES, :], ACT.Square).then_inc(s_sq[0], 1)
            act.wait_ge(s_stat, 1)

            def squares_of_x(b):
                for t in range(TILES):
                    n = TILES * b + t
                    last = nc.scalar.activation(squares(b)[:, t, :], X[:, n, :], ACT.Square,
                                                bias=nmr[:, n:n + 1], scale=rstd[:, n:n + 1])
                last.then_inc(s_sq[b], 1)

            squares_of_x(3)
            act.wait_ge(s_norm, 2)
            nc.scalar.activation(squares(1), XN[:, TILES:2 * TILES, :], ACT.Square).then_inc(s_sq[1], 1)
            squares_of_x(2)
            act.wait_ge(s_bt, 1)
            with act.Fori(0, GROUPS) as g:
                for n in range(UNITS):
                    tile, x = n // 2, n % 2
                    act.wait_ge(s_S, UNITS * g + n + 1)
                    nc.scalar.activation(E[:, tile % SLOTS, 2 * x:2 * x + 2, :].rearrange("p h n -> p (h n)"),
                                         score_ps[n % BANKS], ACT.Exp).then_inc(s_E, 1)

            for f in range(2):
                act.wait_ge(s_tail_t, f + 1)
                nc.scalar.copy(tail_fT[:, f, :], tail_t(f)).then_inc(s_tail_c, 1)
                for c in range(HC):
                    n = HC * f + c
                    act.wait_ge(s_tail_h, n + 1)
                    nc.scalar.activation(tail_r[:, n, :], tail_h(f, c), ACT.Relu).then_inc(s_tail_r, 1)
                    if f == 0 and c % 2 == 1:
                        act.wait_ge(s_tail_r, n + 1)
                        nc.scalar.activation(tail_r2[:, n, :], tail_r[:, n, :], ACT.Square).then_inc(s_tail_r2_act, 1)

        @block.tensor
        def _(pe):
            pe.wait_ge(s_const, 2)
            pe.wait_ge(s_lw, 64)
            nc.tensor.transpose(lr_ps[0:RANK, 0:RANK], fb_sb[:, :], ident[0:RANK, 0:RANK])
            for c in range(HC):
                last = nc.tensor.transpose(lr_ps[0:RANK, HALF + P * c:HALF + P * (c + 1)], u_sb[:, c, :], ident[:, :])
            last.then_inc(s_lt, 1)
            pe.wait_ge(s_lr, 1)
            nc.tensor.matmul(aux_ps[0:RANK, 0:C], fbT[:, :], v_sb[:, :], start=True, stop=True).then_inc(s_lt, 1)
            pe.wait_ge(s_lr, 2)
            nc.tensor.matmul(lr_ps[:, 0:HID], fbv[:, :], uT[:, :], start=True, stop=True).then_inc(s_lt, 1)
            pe.wait_ge(s_norm, 1)
            for t in range(TILES):
                last = nc.tensor.transpose(score_ps[0][:, P * t:P * (t + 1)], XN[:, t, :], ident[:, :])
            last.then_inc(s_xt, 1)
            def warm_up(n):
                for _ in range(n):
                    nc.tensor.matmul(o_ps, split[:, 3, 0:P], split[:, 3, 0:HALF], start=True, stop=True)

            pe.wait_ge(s_wsq[1], 1)
            warm_up(WARM_UP[0])
            pe.wait_ge(s_bt, 1)
            nc.tensor.transpose(aux_ps[0:BOUNDS, 0:P], bounds[:, :], ident[:, :]).then_inc(s_btt, 1)
            pe.wait_ge(s_flag, 1)
            general = pe.value_load(flag[0:1, 0:1], min_val=0, max_val=1)

            def score(k, jt, h, ps, left, right, rows):
                r = h % 2
                for half in range(2):
                    last = nc.tensor.matmul(
                        ps[:, HALF * half:HALF * (half + 1)],
                        left[k][64 * r:64 * r + rows, h // 2, P * jt:P * (jt + 1)],
                        right[k][64 * r:64 * r + rows, h // 2, HALF * half:HALF * (half + 1)],
                        start=True, stop=True, tile_position=(64 * r, 0))
                return last

            with pe.If(general == 1):
                with pe.Fori(0, LATER) as i:
                    pe.wait_ge(general_later[2], i + 1)
                    transpose_later(pe, i, general_later)
                with pe.Fori(0, GROUPS) as g:
                    pe.wait_ge(m_load, PARTS_LOADED * (g + 1))
                    for n in range(HG * TILES):
                        h, it = n // TILES, n % TILES
                        pe.wait_ge(m_max, 32 * g + n + 1)
                        score(0, it, h, score_ps[n % 2], QT, KT, ROWS).then_inc(m_S, 1)
                    pe.wait_ge(m_max, 32 * g + 34)
                    nc.tensor.transpose(aux_ps[0:HG * TILES, 0:P], rmax[:, :, :].rearrange("p h t -> p (h t)"),
                                        ident[:, :]).then_inc(m_t, 1)
                pe.wait_ge(m_load, PARTS_LOADED * (GROUPS + 1) + 64)

            def unit(k, n):
                half, jt, x = n // (2 * TILES), n // 2 % TILES, n % 2
                for r in range(2):
                    last = nc.tensor.matmul(
                        score_ps[n % BANKS][:, HALF * r:HALF * (r + 1)],
                        KT[k][64 * r:64 * r + SROWS, x, P * jt:P * (jt + 1)],
                        QT[k][64 * r:64 * r + SROWS, x, HALF * half:HALF * (half + 1)],
                        start=True, stop=True, tile_position=(64 * r, 0))
                last.then_inc(s_S, 1)

            def pv(k, tile):
                jt = tile % TILES
                for h in range(HG):
                    last = nc.tensor.matmul(
                        o_ps[VW * h:VW * (h + 1), :], V[k][:, jt, h, :], E[:, tile % SLOTS, h, :],
                        start=(jt == 0), stop=(jt == TILES - 1), tile_position=(0, VW * h))
                last.then_inc(s_pv, 1)

            def ffn_transpose(chunk):
                pe.wait_ge(s_fn, chunk + 1)
                for t in range(FT):
                    last = nc.tensor.transpose(aux_ps[:, P * t:P * (t + 1)], fn[:, t, :], ident[:, :])
                last.then_inc(s_fT, 1)

            def ffn_hidden(chunk, c):
                if c == 0:
                    pe.wait_ge(s_fTc, chunk + 1)
                if c == 2:
                    pe.wait_ge(s_relu, 2 * chunk + 1)
                last = nc.tensor.matmul(aux_ps[:, FT * P * (c % 2):FT * P * (c % 2 + 1)], W1[:, P * c:P * (c + 1)],
                                        fT[:, :], start=True, stop=True)
                if c % 2 == 1:
                    last.then_inc(s_fc, 1)

            def ffn_project(chunk, t):
                if t == 0:
                    pe.wait_ge(s_relu2, 2 * chunk + 2)
                for c in range(HC):
                    last = nc.tensor.matmul(aux_ps[:, P * t:P * (t + 1)], relu2[:, c, P * t:P * (t + 1)],
                                            W2[:, c, :], start=(c == 0), stop=(c == HC - 1))
                if t == FT - 1:
                    last.then_inc(s_fp, 1)

            def group(s, k, ffn, last_group=False):
                g = 2 * s + k
                chunk = g - LAG
                for tile in range(SWEEPS * TILES):
                    half, jt = tile // TILES, tile % TILES
                    if tile == 0:
                        pe.wait_ge(s_v[k], s + (1 if k == 0 else 3))
                    if jt == 0:
                        pe.wait_ge(s_ev, 2 * g + half + 1)
                    pv(k, tile)
                    for m in (2 * tile + AHEAD, 2 * tile + AHEAD + 1):
                        if m < UNITS:
                            pe.wait_ge(s_E, UNITS * g + m - 2)
                            unit(k, m)
                        elif not last_group:
                            if m == UNITS:
                                pe.wait_ge(s_first[1], 64)
                                pe.wait_ge(s_qk[1 - k], LOADED * (s + 1 + k))
                            pe.wait_ge(s_E, UNITS * g + {0: 31, 1: 32, 2: 32}.get(m - UNITS, m - 2))
                            unit(1 - k, m - UNITS)
                        else:
                            pe.wait_ge(s_E, UNITS * g + min(m - 2, UNITS))
                    if ffn:
                        if tile == FFN_AT[0]:
                            pe.wait_ge(s_att, 2 * g + 1)
                            ffn_transpose(chunk)
                        for c in range(HC):
                            if tile == FFN_AT[1 + c]:
                                ffn_hidden(chunk, c)
                        for t in range(FT):
                            if tile == FFN_AT[1 + HC + t]:
                                if t == 0:
                                    pe.wait_ge(s_att, 2 * g + 2)
                                ffn_project(chunk, t)
                    else:
                        if tile in (1, 10):
                            pe.wait_ge(s_att, 2 * g + half + 1)
                            transpose_later(pe, SWEEPS * g + half, main_later)
                        if (k, tile) == (1, 5):
                            pe.wait_ge(main_later[2], SWEEPS * g + 2)
                            pe.wait_ge(s_ws, s + 1)
                            for c in range(HC):
                                last = nc.tensor.transpose(aux_ps[:, P * c:P * (c + 1)], staged_w[:, P * c:P * (c + 1)], ident[:, :])
                            last.then_inc(s_wt, 1)
                    if jt == TILES - 1:
                        if ffn and half == 0:
                            pe.wait_ge(s_relu, 2 * chunk + 2)
                        elif ffn:
                            pe.wait_ge(s_y, chunk + 1)
                        elif (k, half) == (1, 0):
                            pe.wait_ge(s_wd, s + 2)
                        else:
                            pe.wait_ge(main_later[2], SWEEPS * g + half + 2)
                        pe.wait_ge(s_ev, 2 * g + half + 2)
                        for t in range(HT):
                            last = nc.tensor.transpose(aux_ps[:, P * t:P * (t + 1)], o_sb[:, P * t:P * (t + 1)], ident[:, :])
                        last.then_inc(s_to, 1)

            warm_up(WARM_UP[1])
            pe.wait_ge(s_first[0], 64)
            pe.wait_ge(s_qk[0], LOADED)
            for n in range(AHEAD):
                if n >= BANKS:
                    warm_up(2)
                    pe.wait_ge(s_E, n - 2)
                unit(0, n)
            with pe.Fori(0, 2) as s:
                for k in range(2):
                    group(s, k, False)
            with pe.Fori(2, STEPS - 1) as s:
                for k in range(2):
                    group(s, k, True)
            group(STEPS - 1, 0, True)
            group(STEPS - 1, 1, True, last_group=True)
            def tail_transpose(f):
                pe.wait_ge(s_tail_n, f + 1)
                for t in range(TAIL):
                    last = nc.tensor.transpose(tail_t(f)[:, P * t:P * (t + 1)], tail_fn[:, TAIL * f + t, :], ident[:, :])
                last.then_inc(s_tail_t, 1)

            def tail_hidden(f):
                pe.wait_ge(s_tail_c, f + 1)
                for c in range(HC):
                    nc.tensor.matmul(tail_h(f, c), W1[:, P * c:P * (c + 1)], tail_fT[:, f, :],
                                     start=True, stop=True).then_inc(s_tail_h, 1)

            def tail_project(f, c):
                if c % 2 == 0:
                    pe.wait_ge(s_tail_r2_pool, 2 * f + c // 2 + 1)
                else:
                    pe.wait_ge((s_tail_r2_act, s_tail_r2_dve)[f], c // 2 + 1)
                for t in range(TAIL):
                    last = nc.tensor.matmul(tail_h(f, 0)[:, P * t:P * (t + 1)], tail_r2[:, HC * f + c, P * t:P * (t + 1)],
                                            W2[:, c, :], start=(c == 0 and t == 0), stop=(c == HC - 1 and t == TAIL - 1))
                if c == HC - 1:
                    last.then_inc(s_tail_p, 1)

            tail_transpose(0)
            tail_hidden(0)
            for c in range(HC - 1):
                tail_project(0, c)
            tail_transpose(1)
            tail_project(0, HC - 1)
            tail_hidden(1)
            for c in range(HC):
                tail_project(1, c)

        class Chain:

            def __init__(self, dve, done, before=0):
                self.dve, self.done, self.before, self.n = dve, done, before, 0

            def then(self, ins):
                ins.then_inc(self.done, 1)
                self.n += 1

            def ready(self):
                self.dve.wait_ge(self.done, self.before + self.n)

            def link(self, ins):
                self.then(ins)
                self.ready()

        def layernorm_rstd(dve, ch, mvs, v, r, t):
            ch.link(nc.vector.tensor_scalar(v, mvs[:, :, 1:2].rearrange("p t o -> p (t o)"), EPS, None, ALU.add))
            ch.link(nc.vector.tensor_scalar(t.bitcast(I32), v.bitcast(I32), 1, None, ALU.logical_shift_right))
            ch.link(nc.vector.tensor_scalar(r.bitcast(I32), t.bitcast(I32), -1.0, MAGIC, ALU.mult, ALU.add))
            for _ in range(3):
                ch.link(nc.vector.scalar_tensor_tensor(out=t, in0=r, scalar=-0.5, in1=r, op0=ALU.mult, op1=ALU.mult))
                ch.link(nc.vector.tensor_tensor(out=t, in0=t, in1=v, op=ALU.mult))
                ch.link(nc.vector.scalar_tensor_tensor(out=r, in0=t, scalar=1.5, in1=r, op0=ALU.add, op1=ALU.mult))

        RSQRT_LINKS = 12

        @block.vector
        def _(dve):
            ch = Chain(dve, c_pre)
            for i, (done, n) in enumerate(((m_max, 2), (m_store, 64), (s_ev, 1), (s_att, 1), (s_qk[0], 32), (s_qk[1], 32), (s_out[0], 16), (s_out[1], 16),
                                           (main_later[1], 1), (main_later[2], 1), (main_later[4], 16),
                                           (general_later[1], 1), (general_later[2], 1), (general_later[4], 16))):
                nc.vector.memset(credit[:, i:i + 1], 0.0).then_inc(done, n)

            def statistics(b):
                dve.wait_ge(s_x[b], 16)
                for t in range(TILES * b, TILES * (b + 1)):
                    ch.then(nc.vector.bn_stats(bn[:, t, :], X[:, t, :]))
                ch.ready()
                for t in range(TILES * b, TILES * (b + 1)):
                    ch.then(nc.vector.bn_aggr(mv[:, t, :], bn[:, t, :]))

            def rstds(b0, b1):
                ch.ready()
                tiles = slice(TILES * b0, TILES * b1)
                layernorm_rstd(dve, ch, mv[:, tiles, :], var[:, tiles], rstd[:, tiles], nt[:, tiles])

            def bound(b):
                dve.wait_ge(s_wsq[b], 1)
                ch.link(nc.vector.tensor_reduce(by_tile[:, :, :], weighted(b).rearrange("p t (h d) -> p t h d", d=D), AX_X, ALU.add))
                ch.link(nc.vector.tensor_reduce(bounds[:, 1 + H * b:1 + H * (b + 1)],
                                                by_tile[:, :, :].rearrange("p t h -> p h t"), AX_X, ALU.max))

            statistics(0)
            rstds(0, 1)
            norm(nc.vector.tensor_scalar, 0, s_norm)
            dve.wait_ge(s_wc, 64)
            ch.then(nc.vector.scalar_tensor_tensor(out=w_c[:, :], in0=rot_c[:, :], scalar=float(D) ** -0.5,
                                                   in1=ent_c[:, :], op0=ALU.mult, op1=ALU.mult))
            ch.link(nc.vector.scalar_tensor_tensor(out=w_r[:, :], in0=rot_r[:, :], scalar=float(D) ** -0.5,
                                                   in1=ent_r[:, :], op0=ALU.mult, op1=ALU.mult))
            nc.vector.scalar_tensor_tensor(out=wabs[:, :], in0=w_r[:, :], scalar=-1.0, in1=w_r[:, :],
                                           op0=ALU.mult, op1=ALU.max).then_inc(s_wabs, 1)
            statistics(1)
            dve.wait_ge(s_split, 2)
            nc.vector.tensor_tensor(out=rest_k[:, :], in0=score_ps[0], in1=split[:, 3, :], op=ALU.subtract).then_inc(s_rest_k, 1)
            statistics(2)
            dve.wait_ge(s_split, 4)
            nc.vector.tensor_tensor(out=split[:, 5, :], in0=rest_k[:, :], in1=split[:, 4, :], op=ALU.subtract).then_inc(s_klow, 1)
            statistics(3)
            rstds(1, B)
            nc.vector.scalar_tensor_tensor(out=nmr[:, TILES:], in0=mv[:, TILES:, 0:1].rearrange("p t o -> p (t o)"),
                                           scalar=-1.0, in1=rstd[:, TILES:], op0=ALU.mult, op1=ALU.mult).then_inc(s_stat, 1)
            norm(nc.vector.tensor_scalar, 1, s_norm)
            bound(0)
            weight_squares(dve, nc.vector.tensor_tensor, 3)
            bound(3)
            bound(1)
            weight_squares(dve, nc.vector.tensor_tensor, 2)
            bound(2)
            nc.vector.tensor_reduce(bounds[:, 0:1], bounds[:, 1:BOUNDS], AX_X, ALU.max).then_inc(s_bt, 1)
            dve.wait_ge(s_btt, 1)
            ch.link(nc.vector.tensor_reduce(bmax[:, :], aux_ps[0:BOUNDS, 0:P], AX_X, ALU.max))
            nc.vector.tensor_scalar(flag[:, :], bmax[0:1, :], SHIFT_LIMIT, None, ALU.is_gt).then_inc(s_flag, 1)
            ch.link(nc.vector.tensor_scalar(bneg[:, :], bmax[:, :], -1.01, -1e-3, ALU.mult, ALU.add))
            dve.wait_ge(s_preset, 2)
            nc.vector.tensor_scalar(shift_row[:, :], zrow[:, :], bneg[:, 0:1], None, ALU.add).then_inc(s_shr, 1)
            dve.wait_ge(s_flag, 1)
            general = dve.value_load(flag[0:1, 0:1], min_val=0, max_val=1)
            for b in (2, 3):
                norm(nc.vector.tensor_scalar, b, s_norm)
            with dve.If(general == 1):
                with dve.Fori(0, LATER) as i:
                    chain = Chain(dve, c_split, SPLIT_LINKS * i)
                    split_later(dve, chain, i, general_later)
                    assert chain.n == SPLIT_LINKS
                with dve.Fori(0, GROUPS) as g:
                    for n in range(HG * TILES):
                        dve.wait_ge(m_S, 32 * g + n + 1)
                        nc.vector.tensor_reduce(rmax[:, n // TILES, n % TILES:n % TILES + 1], score_ps[n % 2],
                                                AX_X, ALU.max).then_inc(m_max, 1)
                    gc = Chain(dve, c_general, 5 * g)
                    dve.wait_ge(m_t, g + 1)
                    gc.link(nc.vector.tensor_scalar(nmax[:, :], aux_ps[0:HG * TILES, 0:P], -1.0, None, ALU.mult))
                    gc.link(nc.vector.tensor_copy(nparts[:, 0, :], nmax[:, :]))
                    gc.link(nc.vector.tensor_tensor(out=nres[:, :], in0=nmax[:, :], in1=nparts[:, 0, :], op=ALU.subtract))
                    gc.link(nc.vector.tensor_copy(nparts[:, 1, :], nres[:, :]))
                    gc.link(nc.vector.tensor_tensor(out=nmax[:, :], in0=nres[:, :], in1=nparts[:, 1, :], op=ALU.subtract))
                    nc.vector.tensor_copy(nparts[:, 2, :], nmax[:, :]).then_inc(m_parts, 1)

            wc = Chain(dve, c_weights)
            dve.wait_ge(s_w, 32)

            def ternary(w, rows, width):
                a = wa[:, :].rearrange("p (t c) -> p t c", t=rows)
                m = wb[:, :].rearrange("p (t c) -> p t c", t=rows)

                def wide(x):
                    return x[:, 0:rows].rearrange("p (t o) -> p t o", o=1).to_broadcast([P, rows, width])

                wc.link(nc.vector.tensor_reduce(ws[:, 0:rows], w, AX_X, ALU.add, apply_absolute_value=True))
                wc.link(nc.vector.tensor_scalar(ws[:, 0:rows], ws[:, 0:rows], 1.0 / width, EPS, ALU.mult, ALU.max))
                wc.then(nc.vector.tensor_scalar(wh[:, 0:rows], ws[:, 0:rows], 0.5, None, ALU.mult))
                wc.link(nc.vector.tensor_scalar(wnh[:, 0:rows], ws[:, 0:rows], -0.5, None, ALU.mult))
                wc.then(nc.vector.tensor_tensor(out=a, in0=w, in1=wide(wh), op=ALU.is_gt))
                wc.link(nc.vector.tensor_tensor(out=m, in0=w, in1=wide(wnh), op=ALU.is_lt))
                wc.link(nc.vector.tensor_tensor(out=a, in0=a, in1=m, op=ALU.subtract))
                wc.link(nc.vector.tensor_tensor(out=m, in0=a, in1=w, op=ALU.subtract))
                wc.link(nc.vector.tensor_tensor(out=a, in0=m, in1=w, op=ALU.add))
                wc.link(nc.vector.tensor_tensor(out=w, in0=a, in1=wide(ws), op=ALU.mult))

            ternary(wfc, HC, C)
            ternary(wpj.rearrange("p (t c) -> p t c", t=1), 1, HID)
            nc.vector.memset(wh[:, :], 0.0).then_inc(s_wd, 1)

            def finish_sweep(chain, s, k, half):
                sweep = SWEEPS * (2 * s + k) + half
                dve.wait_ge(s_pv, TILES * (sweep + 1))
                nc.vector.tensor_copy(o_sb[:, :], o_ps).then_inc(s_ev, 1)
                dve.wait_ge(s_to, sweep + 1)
                heads = aux_ps.rearrange("p (t h v) -> p t h v", t=HT, h=HG)
                chain.link(nc.vector.reciprocal(rden[:, :, :], heads[:, :, :, D:D + 1].rearrange("p t h o -> p t (h o)")))
                nc.vector.tensor_tensor(
                    out=att[:, :, :, :].rearrange("p t h d -> p (t h) d"),
                    in0=aux_ps.rearrange("p (th v) -> p th v", v=VW)[:, :, 0:D],
                    in1=rden[:, :, :].rearrange("p t (h o) -> p (t h) o", o=1).to_broadcast([P, HT * HG, D]),
                    op=ALU.mult).then_inc(s_att, 1)
                dve.wait_ge(s_att, sweep + 2)
                xs = X[:, bass.ds(TILES * (s // 2) + HT * half, HT), bass.ds(64 * (s % 2) + 32 * k, HG * D)]
                chain.link(nc.vector.tensor_tensor(out=xs, in0=xs, in1=att[:, :, :, :].rearrange("p t h d -> p t (h d)"),
                                                   op=ALU.add))

            FINISH_LINKS = 2

            def ffn_hidden(chain, pair, k):
                chunk = 2 * pair + k

                def tile(t):
                    return X[:, bass.ds(FT * chunk + t, 1), :].rearrange("p t c -> p (t c)")

                for t in range(FT):
                    chain.then(nc.vector.bn_stats(fbn[:, t, :], tile(t)))
                chain.ready()
                chain.then(nc.vector.memset(fnt[:, :], 0.0))
                for t in range(FT):
                    chain.then(nc.vector.bn_aggr(fmv[:, t, :], fbn[:, t, :]))
                chain.ready()
                layernorm_rstd(dve, chain, fmv, fvar[:, :], frstd[:, :], fnt[:, :])
                for t in range(FT):
                    last = nc.vector.tensor_scalar(fn[:, t, :], tile(t), fmv[:, t, 0:1], frstd[:, t:t + 1],
                                                   ALU.subtract, ALU.mult)
                last.then_inc(s_fn, 1)
                dve.wait_ge(s_fT, chunk + 1)
                nc.vector.tensor_copy(fT[:, :], aux_ps[:, 0:FT * P]).then_inc(s_fTc, 1)
                for part in range(2):
                    dve.wait_ge(s_fc, 2 * chunk + 1 + part)
                    nc.vector.tensor_scalar(relu[:, 2 * part:2 * part + 2, :].rearrange("p c n -> p (c n)"), aux_ps, 0.0, None,
                                            ALU.max).then_inc(s_relu, 1)

            def ffn_output(pair, k):
                chunk = 2 * pair + k
                dve.wait_ge(s_fp, chunk + 1)
                dve.wait_ge(s_out[k], 16 * pair + 16)
                nc.vector.tensor_tensor(
                    out=y[k][:, :, :], in0=aux_ps[:, 0:FT * P].rearrange("p (t c) -> p t c", c=C),
                    in1=X[:, bass.ds(FT * chunk, FT), :], op=ALU.add).then_inc(s_y, 1)

            FFN_LINKS = 2 * FT + RSQRT_LINKS + 1

            each = SWEEPS * (SPLIT_LINKS + FINISH_LINKS)
            with dve.Fori(0, LAG // 2) as s:
                for k in range(2):
                    chain = Chain(dve, c_first, each * (2 * s + k))
                    for half in range(SWEEPS):
                        split_later(dve, chain, SWEEPS * (2 * s + k) + half, main_later)
                        if (k, half) == (1, 0):
                            dve.wait_ge(s_wt, s + 1)
                            nc.vector.tensor_copy(weights_T[:, bass.ds(s, 1), :].rearrange("p o n -> p (o n)"),
                                                  aux_ps).then_inc(s_wd, 1)
                        finish_sweep(chain, s, k, half)
                    assert chain.n == each
            dve.wait_ge(s_wd, 3)
            dve.wait_ge(s_lr, 3)
            nc.vector.tensor_tensor(out=W1, in0=W1, in1=low_rank[:, :], op=ALU.add)
            each = SWEEPS * FINISH_LINKS + FFN_LINKS

            def ffn_and_group(chain, s, k):
                ffn_hidden(chain, s - LAG // 2, k)
                finish_sweep(chain, s, k, 0)
                ffn_output(s - LAG // 2, k)
                finish_sweep(chain, s, k, 1)

            with dve.Fori(2, STEPS - 1) as s:
                for k in range(2):
                    chain = Chain(dve, c_mid, each * (2 * s + k - LAG))
                    ffn_and_group(chain, s, k)
                    assert chain.n == each
            first, tc = (B - 1) * TILES, Chain(dve, c_tail)

            def tail_norm(f):
                tiles = slice(TAIL * f, TAIL * (f + 1))
                for t in range(TAIL * f, TAIL * (f + 1)):
                    tc.then(nc.vector.bn_stats(bn[:, t, :], X[:, first + t, :]))
                tc.ready()
                tc.then(nc.vector.memset(nt[:, tiles], 0.0))
                for t in range(TAIL * f, TAIL * (f + 1)):
                    tc.then(nc.vector.bn_aggr(mv[:, t, :], bn[:, t, :]))
                tc.ready()
                layernorm_rstd(dve, tc, mv[:, tiles, :], var[:, tiles], rstd[:, tiles], nt[:, tiles])
                for t in range(TAIL * f, TAIL * (f + 1)):
                    last = nc.vector.tensor_scalar(tail_fn[:, t, :], X[:, first + t, :], mv[:, t, 0:1], rstd[:, t:t + 1],
                                                   ALU.subtract, ALU.mult)
                last.then_inc(s_tail_n, 1)

            def tail_output(f):
                dve.wait_ge(s_tail_p, f + 1)
                nc.vector.tensor_tensor(
                    out=tail_y[:, TAIL * f:TAIL * (f + 1), :], in0=tail_h(f, 0).rearrange("p (t c) -> p t c", c=C),
                    in1=X[:, first + TAIL * f:first + TAIL * (f + 1), :], op=ALU.add).then_inc(s_tail_y, 1)

            chain = Chain(dve, c_last)
            ffn_and_group(chain, STEPS - 1, 0)
            ffn_hidden(chain, STEPS - 1 - LAG // 2, 1)
            finish_sweep(chain, STEPS - 1, 1, 0)
            tail_norm(0)
            ffn_output(STEPS - 1 - LAG // 2, 1)
            finish_sweep(chain, STEPS - 1, 1, 1)
            tail_norm(1)
            tail_output(0)
            for n in range(HC + 1, 2 * HC, 2):
                square_tail(dve, nc.vector.tensor_tensor, n, s_tail_r2_dve)
            tail_output(1)


_INS = ["L0_attn_inputs", "L0_attn_rotation_params", "L0_attn_entangle_params", "L0_ffn_fast_b",
        "L0_ffn_w_fc", "L0_ffn_w_proj", "L0_ffn_u", "L0_ffn_v", "L0_ffn_gate"]


def kernel(**inputs):
    import numpy as _np
    import concourse.bacc as _bacc
    from concourse import mybir as _mybir
    from concourse.bass_utils import run_bass_kernel_spmd as _run

    nc = _bacc.Bacc("TRN2", target_bir_lowering=False, num_devices=1)
    arrays, args = {}, []
    for name in _INS:
        a = _np.ascontiguousarray(inputs[name])
        a = a.reshape(1) if a.ndim == 0 else a
        arrays[f"in_{name}_dram"] = a
        args.append(nc.dram_tensor(f"in_{name}_dram", a.shape, _mybir.dt.from_np(a.dtype), kind="ExternalInput").ap())
    args.append(nc.dram_tensor("out_0_dram", (B, T, C), _mybir.dt.float32, kind="ExternalOutput").ap())
    build(nc, *args)
    r = _run(nc, [arrays], core_ids=[0])
    return r.results[0]["out_0_dram"]
```
